# Optimizing a Trainium2 kernel written in Bass

```python
import numpy as np
import jax
import jax.numpy as jnp

def _softmax(x, axis=-1):
    return jax.nn.softmax(x, axis=axis)

def _gelu(x):
    return jax.nn.gelu(x, approximate=True)

def _silu(x):
    return jax.nn.silu(x)

def _sigmoid(x):
    return jax.nn.sigmoid(x)

def _layernorm(x, axis=-1, eps=1e-05):
    m = jnp.mean(x, axis=axis, keepdims=True)
    v = jnp.var(x, axis=axis, keepdims=True)
    return (x - m) / jnp.sqrt(v + eps)

def _scatter_add(tgt, idx, src, axis=0):
    return tgt.at[idx].add(src)

def _segment_sum(src, seg, n):
    return jax.ops.segment_sum(src, seg, n)
kernel_name = 'mk_macaron_d1_jaxref_r8_472744'

def setup_inputs(seed: int=0):
    np.random.seed(seed)
    _w = jnp.asarray

    def _L0_attn_setup():
        import jax, jax.numpy as jnp
        import numpy as np
        D_MODEL = 128
        N_HEADS = 16
        HEAD_DIM = D_MODEL // N_HEADS
        MAX_REL = 128
        B, S = (8, 128)
        key = jax.random.key(seed)
        ks = jax.random.split(key, 12)
        sc = 1.0 / np.sqrt(D_MODEL)
        return {'hidden_states': jax.random.normal(ks[0], (B, S, D_MODEL), jnp.float32), 'Wq': jax.random.normal(ks[1], (D_MODEL, D_MODEL), jnp.float32) * sc, 'bq': jnp.zeros((D_MODEL,), jnp.float32), 'Wk': jax.random.normal(ks[2], (D_MODEL, D_MODEL), jnp.float32) * sc, 'bk': jnp.zeros((D_MODEL,), jnp.float32), 'Wv': jax.random.normal(ks[3], (D_MODEL, D_MODEL), jnp.float32) * sc, 'bv': jnp.zeros((D_MODEL,), jnp.float32), 'Wo': jax.random.normal(ks[4], (D_MODEL, D_MODEL), jnp.float32) * sc, 'bo': jnp.zeros((D_MODEL,), jnp.float32), 'rel_emb': jax.random.normal(ks[5], (2 * MAX_REL + 1, HEAD_DIM), jnp.float32) * 0.02, 'M': jax.random.uniform(ks[6], (N_HEADS, HEAD_DIM, HEAD_DIM), jnp.float32), 'z': jax.random.uniform(ks[7], (N_HEADS, HEAD_DIM), jnp.float32), 'gate_alpha': jnp.float32(0.5)}
    _L0_attn_in = _L0_attn_setup()

    def _L0_ffn_setup():
        import jax, jax.numpy as jnp
        import numpy as np
        TOP_K = 2
        E = 8
        D = 128
        F = 256
        B, S = (2, 128)
        key = jax.random.key(seed)
        ks = jax.random.split(key, 8)
        sc = 0.02
        return {'x_bsD': jax.random.normal(ks[0], (B, S, D), dtype=jnp.float32), 'router_DE': jax.random.normal(ks[1], (D, E), dtype=jnp.float32) * sc, 'w_in_shared_FD': jax.random.normal(ks[2], (F, D), dtype=jnp.float32) * sc, 'w_out_shared_DF': jax.random.normal(ks[3], (D, F), dtype=jnp.float32) * sc, 'w_swiglu_FD': jax.random.normal(ks[4], (F, D), dtype=jnp.float32) * sc, 'w_in_eDF': jax.random.normal(ks[5], (E, D, F), dtype=jnp.float32) * sc, 'w_swiglu_eDF': jax.random.normal(ks[6], (E, D, F), dtype=jnp.float32) * sc, 'w_out_eFD': jax.random.normal(ks[7], (E, F, D), dtype=jnp.float32) * sc}
    _L0_ffn_in = _L0_ffn_setup()
    _d = {'L0_attn_hidden_states': _L0_attn_in['hidden_states'], 'L0_attn_Wq': _L0_attn_in['Wq'], 'L0_attn_bq': _L0_attn_in['bq'], 'L0_attn_Wk': _L0_attn_in['Wk'], 'L0_attn_bk': _L0_attn_in['bk'], 'L0_attn_Wv': _L0_attn_in['Wv'], 'L0_attn_bv': _L0_attn_in['bv'], 'L0_attn_Wo': _L0_attn_in['Wo'], 'L0_attn_bo': _L0_attn_in['bo'], 'L0_attn_rel_emb': _L0_attn_in['rel_emb'], 'L0_attn_M': _L0_attn_in['M'], 'L0_attn_z': _L0_attn_in['z'], 'L0_attn_gate_alpha': _L0_attn_in['gate_alpha'], 'L0_ffn_router_DE': _L0_ffn_in['router_DE'], 'L0_ffn_w_in_shared_FD': _L0_ffn_in['w_in_shared_FD'], 'L0_ffn_w_out_shared_DF': _L0_ffn_in['w_out_shared_DF'], 'L0_ffn_w_swiglu_FD': _L0_ffn_in['w_swiglu_FD'], 'L0_ffn_w_in_eDF': _L0_ffn_in['w_in_eDF'], 'L0_ffn_w_swiglu_eDF': _L0_ffn_in['w_swiglu_eDF'], 'L0_ffn_w_out_eFD': _L0_ffn_in['w_out_eFD']}
    _x0 = _d['L0_attn_hidden_states']
    _d['L0_attn_hidden_states'] = jax.random.normal(jax.random.fold_in(jax.random.key(seed), 1), (16, 512, 128), dtype=_x0.dtype)
    del _x0
    return _d

def reference(L0_attn_hidden_states, L0_attn_Wq, L0_attn_bq, L0_attn_Wk, L0_attn_bk, L0_attn_Wv, L0_attn_bv, L0_attn_Wo, L0_attn_bo, L0_attn_rel_emb, L0_attn_M, L0_attn_z, L0_attn_gate_alpha, L0_ffn_router_DE, L0_ffn_w_in_shared_FD, L0_ffn_w_out_shared_DF, L0_ffn_w_swiglu_FD, L0_ffn_w_in_eDF, L0_ffn_w_swiglu_eDF, L0_ffn_w_out_eFD):

    def _L0_attn_ref(hidden_states, Wq, bq, Wk, bk, Wv, bv, Wo, bo, rel_emb, M, z, gate_alpha):
        import jax, jax.numpy as jnp
        import numpy as np
        D_MODEL = 128
        N_HEADS = 16
        HEAD_DIM = D_MODEL // N_HEADS
        MAX_REL = 128
        B, S = (8, 128)
        b, s, _ = hidden_states.shape

        def proj(W, bias):
            y = hidden_states @ W.T + bias
            return y.reshape(b, s, N_HEADS, HEAD_DIM).transpose(0, 2, 1, 3)
        q = proj(Wq, bq)
        k = proj(Wk, bk)
        v = proj(Wv, bv)
        dist = jnp.arange(s)[:, None] - jnp.arange(s)[None, :]
        dist = jnp.clip(dist, -MAX_REL, MAX_REL) + MAX_REL
        rel_pos = rel_emb[dist]
        scores = jnp.einsum('bhqd,bhkd->bhqk', q, k)
        scores = scores + jnp.einsum('bhqd,qkd->bhqk', q, rel_pos)
        scores = scores / np.sqrt(HEAD_DIM).astype(np.float32)
        attn = jax.nn.softmax(scores, axis=-1)
        local_ctx = jnp.einsum('bhqk,bhkd->bhqd', attn, v)
        sigma_q = jax.nn.elu(q) + 1.0
        num = jnp.einsum('bhqk,hkv->bhqv', sigma_q, M)
        den = jnp.einsum('bhqk,hk->bhq', sigma_q, z) + 1e-06
        global_attn = num / den[..., None]
        gate = jax.nn.sigmoid(gate_alpha)
        combined = gate * local_ctx + (1.0 - gate) * global_attn
        out = combined.transpose(0, 2, 1, 3).reshape(b, s, D_MODEL)
        return out @ Wo.T + bo

    def _L0_ffn_ref(x_bsD, router_DE, w_in_shared_FD, w_out_shared_DF, w_swiglu_FD, w_in_eDF, w_swiglu_eDF, w_out_eFD):
        import jax, jax.numpy as jnp
        import numpy as np
        TOP_K = 2
        E = 8
        D = 128
        F = 256
        B, S = (2, 128)
        b, s, d = x_bsD.shape
        x_aD = x_bsD.reshape(-1, d)
        a = x_aD.shape[0]
        scores_aE = x_aD @ router_DE
        topv_aK, topi_aK = jax.lax.top_k(scores_aE, TOP_K)
        masked_aE = jnp.full_like(scores_aE, -jnp.inf)
        masked_aE = masked_aE.at[jnp.arange(a)[:, None], topi_aK].set(topv_aK)
        gates_Ea = jax.nn.sigmoid(masked_aE.astype(jnp.float32)).astype(x_aD.dtype).T
        routed_in_EaD = x_aD[None, :, :] * gates_Ea[:, :, None]
        routed_in_EaD = jax.lax.stop_gradient(routed_in_EaD)
        mid_EaF = jnp.einsum('ead,edf->eaf', routed_in_EaD, w_in_eDF)
        sw_EaF = jnp.einsum('ead,edf->eaf', routed_in_EaD, w_swiglu_eDF)
        h_EaF = jax.nn.silu(mid_EaF) * sw_EaF
        out_EaD = jnp.einsum('eaf,efd->ead', h_EaF, w_out_eFD)
        shared_aF = jax.nn.silu(x_aD @ w_in_shared_FD.T) * (x_aD @ w_swiglu_FD.T)
        shared_out_aD = jax.lax.stop_gradient(shared_aF @ w_out_shared_DF.T)
        out_aD = shared_out_aD + jnp.sum(out_EaD, axis=0)
        return out_aD.reshape(b, s, d)
    x = L0_attn_hidden_states
    x = x + 0.5 * _L0_ffn_ref(_layernorm(x, axis=-1), L0_ffn_router_DE, L0_ffn_w_in_shared_FD, L0_ffn_w_out_shared_DF, L0_ffn_w_swiglu_FD, L0_ffn_w_in_eDF, L0_ffn_w_swiglu_eDF, L0_ffn_w_out_eFD)
    x = x + _L0_attn_ref(_layernorm(x, axis=-1), L0_attn_Wq, L0_attn_bq, L0_attn_Wk, L0_attn_bk, L0_attn_Wv, L0_attn_bv, L0_attn_Wo, L0_attn_bo, L0_attn_rel_emb, L0_attn_M, L0_attn_z, L0_attn_gate_alpha)
    x = x + 0.5 * _L0_ffn_ref(_layernorm(x, axis=-1), L0_ffn_router_DE, L0_ffn_w_in_shared_FD, L0_ffn_w_out_shared_DF, L0_ffn_w_swiglu_FD, L0_ffn_w_in_eDF, L0_ffn_w_swiglu_eDF, L0_ffn_w_out_eFD)
    return x

_drawn_inputs = setup_inputs


def setup_inputs(seed=0):
    import zlib

    import numpy as np

    out = dict(_drawn_inputs(seed))
    spreads = {'L0_attn_bq': (0.0, 0.707),
     'L0_attn_bk': (0.0, 2.0),
     'L0_attn_bv': (0.0, 0.1),
     'L0_attn_bo': (0.0, 0.1)}
    factors = {'L0_attn_rel_emb': 23.441,
     'L0_ffn_router_DE': 8.0,
     'L0_ffn_w_in_shared_FD': 8.0,
     'L0_ffn_w_out_shared_DF': 8.0,
     'L0_ffn_w_swiglu_FD': 8.0,
     'L0_ffn_w_in_eDF': 8.0,
     'L0_ffn_w_swiglu_eDF': 8.0,
     'L0_ffn_w_out_eFD': 8.0}
    for name, (base, spread) in spreads.items():
        noise = np.random.default_rng([zlib.crc32(name.encode()), seed]).standard_normal(out[name].shape)
        drawn = base * np.exp(spread * noise) if base else spread * noise
        out[name] = jnp.asarray(drawn.astype(out[name].dtype))
    for name, factor in factors.items():
        out[name] = (out[name] * factor).astype(out[name].dtype)
    return out
```

```python
from contextlib import ExitStack

import concourse.bass as bass
from concourse import mybir

P = 128
F32, F32R, BF16, U32 = mybir.dt.float32, mybir.dt.float32r, mybir.dt.bfloat16, mybir.dt.uint32
ALU, ACT, AX = mybir.AluOpType, mybir.ActivationFunctionType, mybir.AxisListType
EPS = 1e-5


class Ring:

    def __init__(self, sem, per):
        self.sem, self.per = sem, per

    def wait(self, eng, n, c):
        if isinstance(n, int) and n * self.per + c <= 0:
            return
        eng.wait_ge(self.sem, n * self.per + c)


def mean_and_variance(dve, STATS, work, done):
    D = P
    STEPS = (
        lambda: dve.tensor_tensor(work[0], STATS[:, :, 1:2], STATS[:, :, 4:5], ALU.add),
        lambda: dve.tensor_tensor(work[1], STATS[:, :, 1:2], STATS[:, :, 4:5], ALU.subtract),
        lambda: dve.tensor_scalar(work[2], work[0], 0.5, None, ALU.mult),
        lambda: dve.tensor_scalar(work[3], work[1], 0.5, None, ALU.mult),
        lambda: dve.tensor_tensor(work[4], work[3], work[3], ALU.mult),
        lambda: dve.tensor_tensor(work[5], STATS[:, :, 2:3], STATS[:, :, 5:6], ALU.add),
        lambda: dve.scalar_tensor_tensor(out=work[6], in0=work[5], scalar=1.0 / D, in1=work[4], op0=ALU.mult, op1=ALU.add),
    )
    for i, step in enumerate(STEPS):
        step().then_inc(done.sem, 1)
        dve.wait_ge(done.sem, i + 1)


def ffn_phase(nc, io, X, STATS, tag, store):
    D, E, F = P, io["router"].shape[1], io["w_in"].shape[2]
    NE, C = E + 1, F // P
    U = NE * C
    T = 4
    N = X.shape[1] // T
    W = T * P
    R = 3
    RH = 6
    RE = 4
    RAW = 8
    DELAY = 3
    NEXT = U - 3
    assert NE % R == 0 and U % RH == 0 and U % 2 == 0 and E % RE == 0

    with ExitStack() as ctx:
        def sb(name, shape, dt):
            return ctx.enter_context(nc.sbuf_tensor(f"{tag}_{name}", shape, dt))

        def ps(name, shape, dt=F32):
            return ctx.enter_context(nc.psum_tensor(f"{tag}_{name}", shape, dt))

        def ring(name, per):
            return Ring(ctx.enter_context(nc.semaphore(f"{tag}_{name}")), per)

        raw = sb("raw", [P, RAW, max(C * D, F)], F32)
        w_mid = sb("w_mid", [P, 2, NE, F], F32R)
        w_gate = sb("w_gate", [P, 2, NE, F], F32R)
        w_out = sb("w_out", [P, 2, NE, C, D], F32R)
        router32 = sb("router32", [P, E], F32)
        router = sb("router", [P, 2, E], F32R)
        ident = sb("ident", [P, P], F32)
        ranks_sb = sb("ranks_sb", [P, T, E], F32)
        ranks = ranks_sb[:]
        rstd = sb("rstd", [P, N * T, 1], F32)
        std = sb("std", [P, N * T, 1], F32)
        eps = sb("eps", [P, 1], F32)
        moments = sb("moments", [P, 7, N * T, 1], F32)
        mean, var = moments[:, 2], moments[:, 6]
        xn = sb("xn", [P, T, D], F32)
        xe = sb("xe", [P, RE, T, D], F32)
        xT_hi = sb("xT_hi", [P, R, W], F32R)
        xT_lo = sb("xT_lo", [P, R, W], F32R)
        silu = sb("silu", [P, RH, W], F32)
        h = sb("h", [P, RH, W], F32)
        h_hi = sb("h_hi", [P, RH, W], F32R)
        h_lo = sb("h_lo", [P, RH, W], F32R)
        scores = sb("scores", [P, T, E], F32)
        tanh = sb("tanh", [P, T, E], F32)
        top = sb("top", [P, 2, T, 1], F32)
        lead = sb("lead", [P, T, 1], F32)
        rest = sb("rest", [P, T, E], F32)
        order = sb("order", [P, T, E], F32)
        pick = sb("pick", [P, 2, T, E], F32)
        gate = sb("gate", [P, T, E], F32)
        oT = sb("oT", [P, W], F32)
        y = sb("y", [P, T, D], F32)

        ps_x = ps("ps_x", [P, 2, W])
        ps_mid = ps("ps_mid", [P, 2, W])
        ps_gate = ps("ps_gate", [P, 2, W])
        ps_out = ps("ps_out", [P, W])
        ps_misc = ps("ps_misc", [P, W])

        const_in = ring("const_in", 0)
        raw_in = [ring(f"raw_in{k}", 0) for k in range(RAW)]
        w_hi = ring("w_hi", 0)
        split = ring("split", 0)
        consts = ring("consts", 0)
        stats_done = ring("stats_done", 0)
        sqrt_done = ring("sqrt_done", 0)
        rstd_done = ring("rstd_done", 0)
        xn_done = ring("xn_done", 1)
        xT_done = ring("xT_done", NE)
        xhi_done = ring("xhi_done", NE)
        xlo_done = ring("xlo_done", NE)
        routed = ring("routed", 1)
        tanh_done = ring("tanh_done", 1)
        chain = ring("chain", 15)
        xe_done = ring("xe_done", E)
        mid_done = ring("mid_done", U)
        silu_done = ring("silu_done", U)
        h_done = ring("h_done", U)
        hhi_done = ring("hhi_done", U)
        hlo_done = ring("hlo_done", U)
        out_done = ring("out_done", U)
        oT_done = ring("oT_done", 1)
        turned = ring("turned", 1)
        y_done = ring("y_done", 2)
        stored = ring("stored", 16)

        block = ctx.enter_context(nc.Block())

        weights = [(io["w_in_s"], w_mid[:, :, 0, :]), (io["w_gate_s"], w_gate[:, :, 0, :]),
                   (io["w_out_s"].rearrange("(c p) d -> p c d", p=P), w_out[:, :, 0])]
        for e in range(E):
            weights += [(io["w_in"][e], w_mid[:, :, e + 1, :]), (io["w_gate"][e], w_gate[:, :, e + 1, :]),
                        (io["w_out"][e].rearrange("(c p) d -> p c d", p=P), w_out[:, :, e + 1])]

        def weights_in(u):
            return [i for i in range(3 + 3 * u // 2 + u % 2, 3 + 3 * (u + 1) // 2 + (u + 1) % 2) if i < len(weights)]

        def shaped(ap, to):
            return ap.rearrange("p (c d) -> p c d", c=C) if len(to.shape) == 4 else ap

        @block.sync
        def _(sp):
            sp.dma_start(router32[:], io["router"]).then_inc(const_in.sem, 16)
            sp.dma_start(ident[:], io["ident"]).then_inc(const_in.sem, 16)
            sp.dma_start(ranks, io["ranks"]).then_inc(const_in.sem, 16)
            for i, (src, to) in enumerate(weights):
                if i >= RAW:
                    sp.wait_ge(split.sem, i - RAW + 1)
                sp.dma_start(shaped(raw[:, i % RAW, :], to), src).then_inc(raw_in[i % RAW].sem, 16)
            if store is not None:
                with sp.Fori(0, N) as n:
                    y_done.wait(sp, n, 2)
                    sp.dma_start(store[:, bass.ts(n, T), :], X[:, bass.ts(n, T), :]).then_inc(stored.sem, 16)
                sp.wait_ge(stored.sem, 16 * N)

        @block.tensor
        def _(pe):
            def product(out, lhs, rhs, start, stop):
                for i, (a, b) in enumerate(((0, 0), (0, 1), (1, 0))):
                    ins = pe.matmul(out, lhs(a), rhs(b), start=start and i == 0, stop=stop and i == 2)
                return ins

            def turn_in(n, e):
                if e == 0:
                    xn_done.wait(pe, n, 1)
                else:
                    xe_done.wait(pe, n, e)
                xlo_done.wait(pe, n, max(e - 1, 0))
                for t in range(T):
                    src = xn[:, t, :] if e == 0 else xe[:, e % RE, t, :]
                    ins = pe.transpose(ps_x[:, e % 2, t * P:(t + 1) * P], src, ident[:])
                ins.then_inc(xT_done.sem, 1)

            def route(n):
                xlo_done.wait(pe, n, 1)
                y_done.wait(pe, n, -3)
                for t in range(T):
                    for i, (a, b) in enumerate(((0, 0), (0, 1), (1, 0), (1, 1))):
                        x = (xT_hi, xT_lo)[a]
                        ins = pe.matmul(ps_misc[:, t * E:(t + 1) * E], x[:, 0, t * P:(t + 1) * P], router[:, b, :],
                                        start=(i == 0), stop=(i == 3))
                ins.then_inc(routed.sem, 1)

            def unit(n, u):
                e, c = divmod(u, C)
                xlo_done.wait(pe, n, e + 1)
                h_done.wait(pe, n, u - 1)
                for w, dst in ((w_mid, ps_mid), (w_gate, ps_gate)):
                    ins = product(dst[:, u % 2, :], lambda a: w[:, a, e, c * P:(c + 1) * P],
                                  lambda b: (xT_hi, xT_lo)[b][:, e % R, :], True, True)
                ins.then_inc(mid_done.sem, 1)

            def output(n, u):
                e, c = divmod(u, C)
                hhi_done.wait(pe, n, u + 1)
                hlo_done.wait(pe, n, u + 1)
                if u == 0:
                    oT_done.wait(pe, n, 0)
                product(ps_out[:], lambda a: w_out[:, a, e, c, :], lambda b: (h_hi, h_lo)[b][:, u % RH, :],
                        u == 0, u == U - 1).then_inc(out_done.sem, 1)

            def turn_out(n):
                oT_done.wait(pe, n, 1)
                chain.wait(pe, n + 1, 1) if n_has_next(n) else None
                for t in range(T):
                    ins = pe.transpose(ps_misc[:, t * P:(t + 1) * P], oT[:, t * P:(t + 1) * P], ident[:])
                ins.then_inc(turned.sem, 1)

            def tile(n, first, last):
                for u in range(U):
                    e, c = divmod(u, C)
                    if u == 4 and not first:
                        turn_out(n - 1)
                    if c == 0 and 1 < e + 1 < NE:
                        turn_in(n, e + 1)
                    if u == NEXT and not last:
                        turn_in(n + 1, 0)
                    if u == NEXT + 1 and not last:
                        route(n + 1)
                    if first:
                        pe.wait_ge(split.sem, 3 * (e + 1))
                    unit(n, u)
                    if u == 1:
                        turn_in(n, 1)
                    if u >= DELAY:
                        output(n, u - DELAY)
                    elif not first:
                        output(n - 1, u - DELAY + U)

            def n_has_next(n):
                return not (isinstance(n, int) and n == N - 1)

            pe.wait_ge(const_in.sem, 48)
            turn_in(0, 0)
            pe.wait_ge(consts.sem, 3)
            route(0)
            tile(0, True, False)
            with pe.Fori(1, N - 1) as n:
                tile(n, False, False)
            tile(N - 1, False, True)
            for u in range(U - DELAY, U):
                output(N - 1, u)
            turn_out(N - 1)

        @block.scalar
        def _(act):
            def x_high(n, e):
                xT_done.wait(act, n, e + 1)
                mid_done.wait(act, n, C * (e - R + 1))
                act.copy(xT_hi[:, e % R, :], ps_x[:, e % 2, :]).then_inc(xhi_done.sem, 1)

            def h_high(n, u):
                h_done.wait(act, n, u + 1)
                out_done.wait(act, n, u - RH + 1)
                act.copy(h_hi[:, u % RH, :], h[:, u % RH, :]).then_inc(hhi_done.sem, 1)

            def leave(n):
                out_done.wait(act, n, U)
                turned.wait(act, n, 0)
                act.copy(oT[:], ps_out[:]).then_inc(oT_done.sem, 1)

            def gates(n):
                chain.wait(act, n, 1)
                act.activation(tanh[:], scores[:], ACT.Tanh, scale=0.5).then_inc(tanh_done.sem, 1)

            def weight_high(i):
                to = weights[i][1]
                act.wait_ge(raw_in[i % RAW].sem, 16 * (i // RAW + 1))
                act.copy(to[:, 0], shaped(raw[:, i % RAW, :], to)).then_inc(w_hi.sem, 1)

            def tile(n, first, last):
                gates(n)
                for u in range(U):
                    e, c = divmod(u, C)
                    if first:
                        for i in weights_in(u):
                            weight_high(i)
                    if u > 0:
                        h_high(n, u - 1)
                    elif not first:
                        h_high(n - 1, U - 1)
                    mid_done.wait(act, n, u + 1)
                    h_done.wait(act, n, u - RH + 1)
                    act.activation(silu[:, u % RH, :], ps_mid[:, u % 2, :], ACT.Silu).then_inc(silu_done.sem, 1)
                    if c == 0 and 1 < e + 1 < NE or u == 1:
                        x_high(n, e + 1)
                    if u == DELAY and not first:
                        leave(n - 1)
                    if u == NEXT and not last:
                        x_high(n + 1, 0)

            act.wait_ge(consts.sem, 1)
            act.wait_ge(stats_done.sem, 7)
            act.activation(std[:], var, ACT.Sqrt, bias=eps[:, 0:1]).then_inc(sqrt_done.sem, 1)
            x_high(0, 0)
            for i in range(3):
                weight_high(i)
            tile(0, True, False)
            with act.Fori(1, N - 1) as n:
                tile(n, False, False)
            tile(N - 1, False, True)
            h_high(N - 1, U - 1)
            leave(N - 1)

        @block.gpsimd
        def _(pool):
            def scale(n, e):
                chain.wait(pool, n, 15)
                xT_done.wait(pool, n, e - RE + 1)
                pool.tensor_tensor(xe[:, e % RE], xn[:], gate[:, :, e - 1:e].broadcast_to([P, T, D]),
                                   ALU.mult).then_inc(xe_done.sem, 1)

            def h_low(n, u):
                hhi_done.wait(pool, n, u + 1)
                out_done.wait(pool, n, u - RH + 1)
                pool.tensor_tensor(h_lo[:, u % RH, :], h[:, u % RH, :], h_hi[:, u % RH, :].bitcast(F32),
                                   ALU.subtract).then_inc(hlo_done.sem, 1)

            def tile(n, first):
                scale(n, 1)
                scale(n, 2)
                for u in range(U):
                    if u > 0:
                        h_low(n, u - 1)
                    elif not first:
                        h_low(n - 1, U - 1)
                    e = (u + 5) // 2
                    if (u + 5) % 2 == 0 and 3 <= e < NE:
                        scale(n, e)

            tile(0, True)
            with pool.Fori(1, N) as n:
                tile(n, False)
            h_low(N - 1, U - 1)

        @block.vector
        def _(dve):
            def normalise(n):
                xe_done.wait(dve, n, 0)
                for t in range(T):
                    r = n * T + t
                    ins = dve.tensor_scalar(xn[:, t, :], X[:, bass.ds(r, 1), :].rearrange("p a d -> p (a d)"),
                                            mean[:, bass.ds(r, 1), :].rearrange("p a d -> p (a d)"),
                                            rstd[:, bass.ds(r, 1), :].rearrange("p a d -> p (a d)"),
                                            ALU.subtract, ALU.mult)
                ins.then_inc(xn_done.sem, 1)

            def x_low(n, e):
                xhi_done.wait(dve, n, e + 1)
                dve.tensor_tensor(xT_lo[:, e % R, :], ps_x[:, e % 2, :], xT_hi[:, e % R, :].bitcast(F32),
                                  ALU.subtract).then_inc(xlo_done.sem, 1)

            def gates(n):
                routed.wait(dve, n, 1)
                xe_done.wait(dve, n, 0)
                dve.tensor_copy(scores[:], ps_misc[:, 0:T * E].rearrange("p (t e) -> p t e", t=T)).then_inc(chain.sem, 1)
                left = scores
                for k in range(2):
                    c = 1 + 6 * k
                    chain.wait(dve, n, c)
                    dve.tensor_reduce(top[:, k], left[:], AX.X, ALU.max).then_inc(chain.sem, 1)
                    chain.wait(dve, n, c + 1)
                    dve.tensor_tensor(pick[:, k], left[:], top[:, k].broadcast_to([P, T, E]), ALU.is_equal).then_inc(chain.sem, 1)
                    chain.wait(dve, n, c + 2)
                    dve.tensor_tensor(order[:], pick[:, k], ranks, ALU.mult).then_inc(chain.sem, 1)
                    chain.wait(dve, n, c + 3)
                    dve.tensor_reduce(lead[:], order[:], AX.X, ALU.max).then_inc(chain.sem, 1)
                    chain.wait(dve, n, c + 4)
                    dve.tensor_tensor(pick[:, k], ranks, lead[:].broadcast_to([P, T, E]), ALU.is_equal).then_inc(chain.sem, 1)
                    chain.wait(dve, n, c + 5)
                    if k == 0:
                        dve.scalar_tensor_tensor(out=rest[:], in0=pick[:, 0], scalar=-3e38, in1=scores[:],
                                                 op0=ALU.mult, op1=ALU.add).then_inc(chain.sem, 1)
                        left = rest
                    else:
                        dve.tensor_tensor(order[:], pick[:, 0], pick[:, 1], ALU.add).then_inc(chain.sem, 1)
                tanh_done.wait(dve, n, 1)
                dve.tensor_scalar(tanh[:], tanh[:], 0.5, 0.5, ALU.mult, ALU.add).then_inc(chain.sem, 1)
                chain.wait(dve, n, 14)
                dve.tensor_tensor(gate[:], tanh[:], order[:], ALU.mult).then_inc(chain.sem, 1)

            def residual(n):
                turned.wait(dve, n, 1)
                rows = X[:, bass.ds(n * T, T), :].rearrange("p t d -> p (t d)")
                flat = y[:].rearrange("p t d -> p (t d)")
                dve.scalar_tensor_tensor(out=flat, in0=ps_misc[:], scalar=0.5, in1=rows, op0=ALU.mult,
                                         op1=ALU.add).then_inc(y_done.sem, 1)
                y_done.wait(dve, n, 1)
                dve.tensor_scalar(rows, flat, 0.0, None, ALU.add).then_inc(y_done.sem, 1)
                for t in range(T):
                    dve.bn_stats(STATS[:, bass.ds(n * T + t, 1), :].rearrange("p a d -> p (a d)"), y[:, t, :])

            def weight_low(i):
                to = weights[i][1]
                dve.wait_ge(w_hi.sem, i + 1)
                dve.tensor_tensor(to[:, 1], shaped(raw[:, i % RAW, :], to), to[:, 0].bitcast(F32),
                                  ALU.subtract).then_inc(split.sem, 1)

            def tile(n, first, last):
                gates(n)
                for u in range(U):
                    e, c = divmod(u, C)
                    if first:
                        for i in weights_in(u):
                            weight_low(i)
                    silu_done.wait(dve, n, u + 1)
                    hhi_done.wait(dve, n, u - RH + 1)
                    hlo_done.wait(dve, n, u - RH + 1)
                    dve.tensor_tensor(h[:, u % RH, :], silu[:, u % RH, :], ps_gate[:, u % 2, :],
                                      ALU.mult).then_inc(h_done.sem, 1)
                    if c == 0 and 1 < e + 1 < NE or u == 1:
                        x_low(n, e + 1)
                    if u == 5 and not first:
                        residual(n - 1)
                    if u == NEXT - 2 and not last:
                        normalise(n + 1)
                    if u == NEXT and not last:
                        x_low(n + 1, 0)

            dve.memset(eps[:], EPS).then_inc(consts.sem, 1)
            mean_and_variance(dve, STATS, [moments[:, i] for i in range(7)], stats_done)
            dve.wait_ge(sqrt_done.sem, 1)
            dve.reciprocal(rstd[:], std[:]).then_inc(rstd_done.sem, 1)
            dve.wait_ge(rstd_done.sem, 1)
            normalise(0)
            dve.wait_ge(const_in.sem, 48)
            for b in range(2):
                if b == 0:
                    dve.tensor_copy(router[:, 0, :], router32[:]).then_inc(consts.sem, 1)
                else:
                    dve.wait_ge(consts.sem, 2)
                    dve.tensor_tensor(router[:, 1, :], router32[:], router[:, 0, :].bitcast(F32), ALU.subtract).then_inc(consts.sem, 1)
            x_low(0, 0)
            for i in range(3):
                weight_low(i)
            tile(0, True, False)
            with dve.Fori(1, N - 1) as n:
                tile(n, False, False)
            tile(N - 1, False, True)
            residual(N - 1)


def attention_phase(nc, io, X, STATS):
    D = X.shape[2]
    H, HD = io["M"].shape[0], io["M"].shape[1]
    Q = X.shape[1]
    QPB = 4
    S = QPB * P
    B = Q // QPB
    COLS = P * H
    REL = (io["rel"].shape[1] - 1) // 2
    SCALE = float(HD) ** -0.5
    OCT = P // H
    NO = P // OCT
    JB = COLS // 512
    IB = P // JB
    PAR = ((1, 1), (1, 2), (2, 1), (2, 2), (1, 3), (3, 1))
    ODD = 64
    KR = ODD + len(PAR) * HD
    KM = KR + 2
    WIN = 2 * S
    VW = H * (HD + 1) + 32 - (HD + 1) + 1
    R2, RQ = 2, 4
    UNROLL = 8

    with ExitStack() as ctx:
        def sb(name, shape, dt=F32):
            return ctx.enter_context(nc.sbuf_tensor(f"at_{name}", shape, dt))

        def ps(name, shape, dt=F32):
            return ctx.enter_context(nc.psum_tensor(f"at_{name}", shape, dt))

        def ring(name, per):
            return Ring(ctx.enter_context(nc.semaphore(f"at_{name}")), per)

        ident = sb("ident", [P, P])
        identb = sb("identb", [P, P], BF16)
        wq, wk, wv, wo = (sb(w, [P, D]) for w in ("wq", "wk", "wv", "wo"))
        bq, bk = sb("bq", [P, 1]), sb("bk", [P, 1])
        bv, bo, ones = sb("bv", [1, D]), sb("bo", [1, D]), sb("ones", [1, P])
        head_of = sb("head_of", [P, H])
        spread = sb("spread", [P, 3, KR], BF16)
        spread32 = sb("spread32", [P, 3, KR])
        pick = sb("pick", [P, H, 3, KR], BF16)
        emb_part = sb("emb_part", [P, 4])
        window = sb("window", [P, WIN], BF16)
        mz = sb("mz", [P, D + H])
        m_sb, z_sb = sb("m_sb", [P, HD]), sb("z_sb", [P, 1])
        gate = sb("gate", [P, 4])
        gate1 = sb("gate1", [P, 1])
        eps = sb("eps", [P, 1])
        moments = sb("moments", [P, 7, Q, 1])
        mean, var = moments[:, 2], moments[:, 6]
        std, rstd = sb("std", [P, Q, 1]), sb("rstd", [P, Q, 1])
        xn = sb("xn", [P, QPB, D])
        xT = sb("xT", [P, S])
        q32 = sb("q32", [P, S])
        rest = sb("rest", [P, S])
        q_hi, q_lo = sb("q_hi", [P, R2, S], F32R), sb("q_lo", [P, R2, S], F32R)
        q_part = sb("q_part", [P, R2, 3, S], BF16)
        k_hi, k_lo = sb("k_hi", [P, R2, S], F32R), sb("k_lo", [P, R2, S], F32R)
        v = sb("v", [P, R2, QPB, VW])
        neg, eneg = sb("neg", [P, S]), sb("eneg", [P, S])
        sigma = sb("sigma", [P, R2, S])
        qd_hi = sb("qd_hi", [P, R2, P, H], F32R)
        qd_lo = sb("qd_lo", [P, P, H], F32R)
        qr = sb("qr", [P, RQ, COLS], BF16)
        nm = sb("nm", [P, NO])
        nm_part = sb("nm_part", [P, 2, NO], BF16)
        nmT = sb("nmT", [2 * NO, P], BF16)
        probs = sb("probs", [P, R2, QPB, H, P])
        oc = sb("oc", [P, 512])
        rden = sb("rden", [P, H, 1])
        rdeng = sb("rdeng", [P, H, 1])
        gden = sb("gden", [P, H, 1])
        grden = sb("grden", [P, H, 1])
        grdeng = sb("grdeng", [P, H, 1])
        local, glob, mixed, mixedT = (sb(x, [P, D]) for x in ("local", "glob", "mixed", "mixedT"))
        y = sb("y", [P, D])

        ps_s = ps("ps_s", [P, 2, 512])
        ps_t = ps("ps_t", [P, 2, 2, 512])
        ps_v = ps("ps_v", [P, 512])
        misc = ps("misc", [P, 512])
        miscb = misc[:].bitcast(BF16)

        const_in, emb_in, zero, step, stats_done = (ring(x, 0) for x in ("const_in", "emb_in", "zero", "step", "stats_done"))
        loads = [(ident[:], io["ident"]), (wq[:], io["wq"]), (wk[:], io["wk"]), (wv[:], io["wv"]), (wo[:], io["wo"]),
                 (bq[:], io["bq"]), (bk[:], io["bk"]), (bv[:], io["bv"]), (bo[:], io["bo"]),
                 (head_of[:], io["head_of"]), (spread32[:], io["spread"]), (emb_part[:], io["emb_part"]),
                 (m_sb[:], io["M"].rearrange("h d v -> (h d) v")), (z_sb[:], io["z"]), (gate[:, 0:1], io["alpha"])]
        stage = probs[:, 0, 0].rearrange("p h i -> p (h i)")[:, 0:WIN]
        parts = [qr[:, 0, 0:WIN], qr[:, 0, WIN:2 * WIN], qr[:, 1, 0:WIN]]
        with nc.Block() as block:
            @block.sync
            def _(sp):
                for to, src in loads:
                    sp.dma_start(to, src).then_inc(const_in.sem, 16)
                sp.wait_ge(zero.sem, 1)
                for par in range(2):
                    for c in range(len(PAR)):
                        r = ODD * par + HD * c
                        at = S - REL + par
                        sp.dma_start(stage[r:r + HD, at:at + 2 * REL + 1], io["rel"]).then_inc(emb_in.sem, 16)

            @block.scalar
            def _(act):
                act.wait_ge(const_in.sem, 16 * len(loads))
                act.wait_ge(zero.sem, 2)
                act.wait_ge(stats_done.sem, 7)
                act.activation(std[:], var, ACT.Sqrt, bias=eps[:, 0:1]).then_inc(step.sem, 1)
                act.activation(gate[:, 1:2], gate[:, 0:1], ACT.Exp, scale=-1.0).then_inc(step.sem, 1)

            @block.vector
            def _(dve):
                dve.memset(stage, 0.0).then_inc(zero.sem, 1)
                dve.memset(eps[:], EPS).then_inc(zero.sem, 1)
                dve.memset(v[:], 1.0).then_inc(zero.sem, 1)
                dve.memset(ones[:], 1.0)
                mean_and_variance(dve, STATS, [moments[:, i] for i in range(7)], stats_done)
                dve.wait_ge(const_in.sem, 16 * len(loads))
                dve.tensor_copy(identb[:], ident[:])
                dve.tensor_copy(spread[:], spread32[:]).then_inc(zero.sem, 1)
                dve.wait_ge(zero.sem, 4)
                for h in range(H):
                    dve.tensor_scalar(pick[:, h], spread[:], head_of[:, h:h + 1], None, ALU.mult)
                mzv = mz[:, 0:D].rearrange("p (h v) -> p h v", h=H)
                dve.tensor_tensor(mzv, head_of[:].rearrange("p (h a) -> p h a", a=1).broadcast_to([P, H, HD]),
                                  m_sb[:].rearrange("p (a v) -> p a v", a=1).broadcast_to([P, H, HD]), ALU.mult)
                dve.tensor_scalar(mz[:, D:D + H], head_of[:], z_sb[:, 0:1], None, ALU.mult)
                dve.wait_ge(step.sem, 2)
                dve.reciprocal(rstd[:], std[:])
                dve.tensor_scalar(gate1[:], gate[:, 1:2], 1.0, None, ALU.add).then_inc(zero.sem, 1)
                dve.wait_ge(zero.sem, 5)
                dve.reciprocal(gate[:, 2:3], gate1[:]).then_inc(zero.sem, 1)
                dve.wait_ge(zero.sem, 6)
                dve.tensor_scalar(gate[:, 3:4], gate[:, 2:3], -1.0, 1.0, ALU.mult, ALU.add)
                dve.wait_ge(emb_in.sem, 16 * 2 * len(PAR))
                for par in range(2):
                    rows = slice(ODD * par, ODD * par + HD * len(PAR))
                    at = S - REL + par
                    dve.tensor_scalar(stage[rows, 0:at], stage[rows, 0:at], stage[rows, at:at + 1], None, ALU.add)
                    dve.tensor_scalar(stage[rows, at + 2 * REL + 1:WIN], stage[rows, at + 2 * REL + 1:WIN],
                                      stage[rows, at + 2 * REL:at + 2 * REL + 1], None, ALU.add).then_inc(zero.sem, 1)
                k = 8
                for i in range(3):
                    dve.wait_ge(zero.sem, k)
                    dve.tensor_copy(parts[i], stage).then_inc(zero.sem, 1)
                    dve.wait_ge(zero.sem, k + 1)
                    dve.tensor_tensor(stage, stage, parts[i], ALU.subtract).then_inc(zero.sem, 1)
                    k += 2
                dve.wait_ge(zero.sem, k)
                dve.tensor_scalar(window[:], parts[0], emb_part[:, 0:1], emb_part[:, 3:4], ALU.mult, ALU.add).then_inc(zero.sem, 1)
                for i in (1, 2):
                    dve.wait_ge(zero.sem, k + i)
                    dve.scalar_tensor_tensor(out=window[:], in0=parts[i], scalar=emb_part[:, i:i + 1], in1=window[:],
                                             op0=ALU.mult, op1=ALU.add).then_inc(zero.sem, 1)
                dve.wait_ge(zero.sem, k + 3)
                dve.memset(qr[:].rearrange("p r c -> p (r c)").bitcast(U32), 0)

        xn_done = ring("xn_done", 1)
        xT_turned = ring("xT_turned", 1)
        xT_done = ring("xT_done", 1)
        q_proj, k_proj, v_proj = (ring(x, 1) for x in ("q_proj", "k_proj", "v_proj"))
        qhi_done = ring("qhi_done", 1)
        q32_done = ring("q32_done", 1)
        qlo_done = ring("qlo_done", 1)
        split = ring("split", 6)
        neg_exp = ring("neg_exp", 1)
        khi_done, klo_done = ring("khi_done", 1), ring("klo_done", 1)
        v_done = ring("v_done", 1)
        rows_done = ring("rows_done", 4)
        even_done = ring("even_done", 4)
        odd_done = ring("odd_done", 4)
        qdhi_done = ring("qdhi_done", JB)
        qdlo_done = ring("qdlo_done", JB)
        s_done = ring("s_done", NO)
        max_done = ring("max_done", NO)
        nm_step = ring("nm_step", 2)
        nm_turned = ring("nm_turned", 1)
        nmT_done = ring("nmT_done", 1)
        nm_in = ring("nm_in", 32)
        t_done = ring("t_done", 2 * JB)
        exp_done = ring("exp_done", 2 * JB)
        pv_done = ring("pv_done", 1)
        oc_done = ring("oc_done", 1)
        o_turned = ring("o_turned", 1)
        o_step = ring("o_step", 3)
        g_prod = ring("g_prod", 1)
        g_step = ring("g_step", 5)
        mixed_turned = ring("mixed_turned", 1)
        mixedT_done = ring("mixedT_done", 1)
        y_prod = ring("y_prod", 1)
        y_done = ring("y_done", 1)

        block = ctx.enter_context(nc.Block())

        def run(eng, step_of):
            first, loops = UNROLL - 3, (Q - UNROLL) // UNROLL
            for c in range(-3, first):
                step_of(0, c)
            with eng.Fori(0, loops) as it:
                for c in range(first, first + UNROLL):
                    step_of(it, c)
            for c in range(first + loops * UNROLL, Q + 2):
                step_of(0, c)

        def at(it, c):
            if isinstance(it, int):
                return c if 0 <= c < Q else None
            return it * UNROLL + c

        def seq(it, c):
            return c // QPB if isinstance(it, int) else it * (UNROLL // QPB) + c // QPB

        def projected(it, c):
            if c % QPB != 1 or at(it, c + 3) is None:
                return None
            return seq(it, c + 3)

        USES = [("A", 0, 0, 0), ("P", 0, 0, 1), ("E", 0, 1, 0), ("P", 1, 1, 1), ("A", 1, 2, 0), ("P", 2, 2, 1),
                ("E", 1, 3, 0), ("P", 3, 3, 1), ("A", 2, 4, 0), ("M", 0, 5, 0), ("E", 2, 5, 1), ("A", 3, 6, 0),
                ("E", 3, 7, 0)]

        def present(it, c, kind):
            return {"A": at(it, c + 2), "P": projected(it, c), "M": at(it, c + 1), "E": at(it, c - 2)}[kind] is not None

        def misc_free(pe, it, c, use):
            i = USES.index(use)
            while True:
                i -= 1
                if i < 0:
                    i, c = len(USES) - 1, c - 1
                    if c < -3:
                        return
                kind, k = USES[i][:2]
                if present(it, c, kind):
                    break
            if kind == "A":
                even_done.wait(pe, at(it, c + 2), k + 1)
                odd_done.wait(pe, at(it, c + 2), k + 1)
            elif kind == "M":
                nmT_done.wait(pe, at(it, c + 1), 1)
            elif kind == "E":
                q = at(it, c - 2)
                [lambda: o_step.wait(pe, q, 3), lambda: g_step.wait(pe, q, 4), lambda: mixedT_done.wait(pe, q, 1),
                 lambda: y_done.wait(pe, q, 1)][k]()
            else:
                b = projected(it, c)
                if k == 0:
                    xT_done.wait(pe, b, 1)
                elif k == 1:
                    qhi_done.wait(pe, b, 1)
                    q32_done.wait(pe, b, 1)
                elif k == 2:
                    klo_done.wait(pe, b, 1)
                else:
                    v_done.wait(pe, b, 1)

        @block.sync
        def _(sp):
            def one(it, c):
                q = at(it, c + 1)
                if q is not None:
                    nmT_done.wait(sp, q, 1)
                    for part in range(2):
                        dst = qr[KR + part:KR + part + 1, (c + 1) % RQ, :]
                        sp.dma_start(dst, nmT[part * NO:(part + 1) * NO, :]).then_inc(nm_in.sem, 16)
            run(sp, one)
            nm_in.wait(sp, Q, 0)

        @block.tensor
        def _(pe):
            def use_a(it, c, k):
                q, b, r = at(it, c), seq(it, c), c // QPB % R2
                split.wait(pe, b, 6)
                i0 = c % QPB * P
                for g in range(4):
                    for part in range(3):
                        ins = pe.matmul(misc[0:KR, g * P:(g + 1) * P], pick[:, 4 * k + g, part, :],
                                        q_part[:, r, part, i0:i0 + P], start=(part == 0), stop=(part == 2))
                ins.then_inc(rows_done.sem, 1)

            def use_p(it, c, b, k):
                if k == 0:
                    xn_done.wait(pe, b, 1)
                    for t in range(QPB):
                        ins = pe.transpose(misc[:, t * P:(t + 1) * P], xn[:, t, :], ident[:])
                    ins.then_inc(xT_turned.sem, 1)
                elif k < 3:
                    xT_done.wait(pe, b, 1)
                    pe.matmul(misc[:], (wq, wk)[k - 1][:], xT[:], start=True, stop=True).then_inc(
                        (q_proj, k_proj)[k - 1].sem, 1)
                else:
                    for t in range(QPB):
                        pe.matmul(misc[:, t * P:(t + 1) * P], xT[:, t * P:(t + 1) * P], wv[:], start=True, stop=False)
                        ins = pe.matmul(misc[:, t * P:(t + 1) * P], ones[:], bv[:], start=False, stop=True)
                    ins.then_inc(v_proj.sem, 1)

            def use_m(q):
                nm_step.wait(pe, q, 2)
                pe.transpose(miscb[0:2 * NO, 0:P], nm_part[:].rearrange("p a o -> p (a o)"), identb[:]).then_inc(nm_turned.sem, 1)

            def use_e(it, c, k):
                q, b, r = at(it, c), seq(it, c), c // QPB % R2
                i0 = c % QPB * P
                if k == 0:
                    oc_done.wait(pe, q, 1)
                    for s in range(4):
                        ins = pe.transpose(misc[:, s * P:(s + 1) * P], oc[:, s * P:(s + 1) * P], ident[:])
                    ins.then_inc(o_turned.sem, 1)
                elif k == 1:
                    pe.matmul(misc[:, 0:D + H], sigma[:, r, i0:i0 + P], mz[:], start=True, stop=True).then_inc(g_prod.sem, 1)
                elif k == 2:
                    g_step.wait(pe, q, 5)
                    pe.transpose(misc[:, 0:D], mixed[:], ident[:]).then_inc(mixed_turned.sem, 1)
                else:
                    mixedT_done.wait(pe, q, 1)
                    pe.matmul(misc[:, 0:D], mixedT[:], wo[:], start=True, stop=False)
                    pe.matmul(misc[:, 0:D], ones[:], bo[:], start=False, stop=True).then_inc(y_prod.sem, 1)

            def scores(it, c, o):
                q, b, r = at(it, c), seq(it, c), c // QPB % R2
                qdhi_done.wait(pe, q, o * OCT // IB + 1)
                if o == 0:
                    klo_done.wait(pe, b, 1)
                    even_done.wait(pe, q, 4)
                    odd_done.wait(pe, q, 4)
                max_done.wait(pe, q, o - 1)
                dst = ps_s[:, o % 2, :]
                pe.matmul(dst, qd_hi[:, c % R2, o * OCT:(o + 1) * OCT, :].rearrange("p i h -> p (i h)"), k_hi[:, r, :],
                          start=True, stop=False, skip_group_check=True)
                for pair in range(4):
                    i = o * OCT + 2 * pair
                    y = S - (c % QPB * P + i)
                    ins = pe.matmul(dst[32 * pair:32 * pair + 32], qr[0:KR, c % RQ, i * H:(i + 2) * H],
                                    window[0:KR, y:y + S], start=False, stop=(pair == 3), skip_group_check=True)
                ins.then_inc(s_done.sem, 1)

            def transposed(it, c, j, kk):
                q, r = at(it, c), c // QPB % R2
                jb, kb = j // 2, j % 2 * 2 + kk
                if kk == 0:
                    qdlo_done.wait(pe, q, jb + 1)
                    exp_done.wait(pe, q, j - 1)
                    if j == 0:
                        nm_in.wait(pe, q, 32)
                dst = ps_t[:, j % 2, kk, :]
                hi = qd_hi[:, c % R2, jb * IB:(jb + 1) * IB, :].rearrange("p i h -> p (i h)")
                lo = qd_lo[:, jb * IB:(jb + 1) * IB, :].rearrange("p i h -> p (i h)")
                keys = slice(kb * P, kb * P + P)
                pe.matmul(dst, k_hi[:, r, keys], hi, start=True, stop=False, skip_group_check=True)
                pe.matmul(dst, k_hi[:, r, keys], lo, start=False, stop=False, skip_group_check=True)
                pe.matmul(dst, k_lo[:, r, keys], hi, start=False, stop=False, skip_group_check=True)
                for pair in range(IB // 2):
                    i = jb * IB + 2 * pair
                    y = S + kb * P - (c % QPB * P + i)
                    ins = pe.matmul(dst[:, 2 * pair * H:2 * (pair + 1) * H], window[0:KM, y:y + P],
                                    qr[0:KM, c % RQ, i * H:(i + 2) * H], start=False, stop=(pair == IB // 2 - 1),
                                    skip_group_check=True)
                if kk == 1:
                    ins.then_inc(t_done.sem, 1)

            def values(it, c, j):
                q, b, r = at(it, c), seq(it, c), c // QPB % R2
                s, half = divmod(j, 2)
                if j == 0:
                    exp_done.wait(pe, q, 2 * JB)
                    v_done.wait(pe, b, 1)
                    oc_done.wait(pe, q, 0)
                for kb in (2 * half, 2 * half + 1):
                    for g in range(4):
                        h = 4 * s + g
                        ins = pe.matmul(ps_v[32 * g:32 * g + 32, s * P:(s + 1) * P],
                                        v[:, r, kb, h * (HD + 1):h * (HD + 1) + 32], probs[:, c % R2, kb, h, :],
                                        start=(kb == 0), stop=(kb == QPB - 1))
                if j == 7:
                    ins.then_inc(pv_done.sem, 1)

            def one(it, c):
                def misc_use(slot, half):
                    for use in USES:
                        if use[2:] == (slot, half) and present(it, c, use[0]):
                            misc_free(pe, it, c, use)
                            kind, k = use[:2]
                            if kind == "A":
                                use_a(it, c + 2, k)
                            elif kind == "P":
                                use_p(it, c, projected(it, c), k)
                            elif kind == "M":
                                use_m(at(it, c + 1))
                            else:
                                use_e(it, c - 2, k)
                for j in range(2 * JB):
                    for half in range(2):
                        misc_use(j, half)
                        if j < 4 and at(it, c + 1) is not None:
                            scores(it, c + 1, 4 * j + 2 * half)
                            scores(it, c + 1, 4 * j + 2 * half + 1)
                        if at(it, c) is not None:
                            transposed(it, c, j, half)
                    if at(it, c - 1) is not None:
                        values(it, c - 1, j)
            run(pe, one)

        @block.scalar
        def _(act):
            def one(it, c):
                for j in range(2 * JB):
                    for kind, k, slot, half in USES:
                        if slot != j or not present(it, c, kind):
                            continue
                        if kind == "A":
                            q = at(it, c + 2)
                            rows_done.wait(act, q, k + 1)
                            if k == 0:
                                t_done.wait(act, q, -2 * JB * (RQ - 1))
                            src = misc[0:len(PAR) * HD, :].rearrange("p (g i two) -> p g i two", g=4, two=2)[:, :, :, 0]
                            dst = qr[0:len(PAR) * HD, (c + 2) % RQ, :].rearrange("p (i two h) -> p h i two", two=2, h=H)
                            act.copy(dst[:, 4 * k:4 * k + 4, :, 0], src).then_inc(even_done.sem, 1)
                        elif kind == "P":
                            b = projected(it, c)
                            r = (c + 3) // QPB % R2
                            if k == 0:
                                xT_turned.wait(act, b, 1)
                                v_proj.wait(act, b, 0)
                                act.copy(xT[:], misc[:]).then_inc(xT_done.sem, 1)
                            elif k == 1:
                                q_proj.wait(act, b, 1)
                                qdhi_done.wait(act, at(it, c + 3), -JB * QPB)
                                act.activation(q_hi[:, r, :], misc[:], ACT.Identity, bias=bq[:, 0:1]).then_inc(qhi_done.sem, 1)
                            elif k == 2:
                                k_proj.wait(act, b, 1)
                                t_done.wait(act, at(it, c + 3), -2 * JB * QPB)
                                act.activation(k_hi[:, r, :], misc[:], ACT.Identity, bias=bk[:, 0:1]).then_inc(khi_done.sem, 1)
                            else:
                                v_proj.wait(act, b, 1)
                                pv_done.wait(act, at(it, c + 3), -QPB)
                                dst = v[:, r, :, 0:H * (HD + 1)].rearrange("p t (h e) -> p t h e", h=H)[:, :, :, 0:HD]
                                act.copy(dst, misc[:].rearrange("p (t h e) -> p t h e", t=QPB, h=H)).then_inc(v_done.sem, 1)
                        elif kind == "E" and k == 2:
                            q = at(it, c - 2)
                            mixed_turned.wait(act, q, 1)
                            y_prod.wait(act, q, 0)
                            act.copy(mixedT[:], misc[:, 0:D]).then_inc(mixedT_done.sem, 1)
                    if j == 6 and projected(it, c) is not None:
                        b = projected(it, c)
                        split.wait(act, b, 5)
                        act.activation(eneg[:], neg[:], ACT.Exp).then_inc(neg_exp.sem, 1)
                    q = at(it, c)
                    if q is not None:
                        t_done.wait(act, q, j + 1)
                        if j == 0:
                            pv_done.wait(act, q, -1)
                        jb, half = divmod(j, 2)
                        dst = probs[:, c % R2, 2 * half:2 * half + 2, :, jb * IB:(jb + 1) * IB].rearrange("p k h i -> p k i h")
                        act.activation(dst, ps_t[:, j % 2].rearrange("p k (i h) -> p k i h", h=H), ACT.Exp,
                                       scale=SCALE).then_inc(exp_done.sem, 1)
            run(act, one)

        @block.gpsimd
        def _(pool):
            heads = head_of[:].rearrange("p (a h) -> p a h", a=1).broadcast_to([P, IB, H])

            def expand(it, c, jb, src, dst, done):
                i0 = c % QPB * P + jb * IB
                x = src[:, c // QPB % R2, i0:i0 + IB].bitcast(F32).rearrange("p (i a) -> p i a", a=1).broadcast_to([P, IB, H])
                pool.tensor_tensor(dst, x, heads, ALU.mult).then_inc(done.sem, 1)

            def one(it, c):
                b = projected(it, c)
                for jb in range(JB):
                    q = at(it, c + 2)
                    if q is not None:
                        qhi_done.wait(pool, seq(it, c + 2), 1)
                        t_done.wait(pool, q, -4 * JB + 2 * jb + 2)
                        expand(it, c + 2, jb, q_hi, qd_hi[:, c % R2, jb * IB:(jb + 1) * IB, :], qdhi_done)
                    q = at(it, c + 1)
                    if q is not None:
                        qlo_done.wait(pool, seq(it, c + 1), 1)
                        t_done.wait(pool, q, -2 * JB + 2 * jb + 2)
                        expand(it, c + 1, jb, q_lo, qd_lo[:, jb * IB:(jb + 1) * IB, :], qdlo_done)
                if b is not None:
                    r = (c + 3) // QPB % R2
                    q32_done.wait(pool, b, 1)
                    qhi_done.wait(pool, b, 1)
                    pool.tensor_tensor(q_lo[:, r, :], q32[:], q_hi[:, r, :].bitcast(F32), ALU.subtract).then_inc(qlo_done.sem, 1)
            run(pool, one)

        @block.vector
        def _(dve):
            def use_a(it, c, k):
                q = at(it, c)
                rows_done.wait(dve, q, k + 1)
                if k == 0:
                    t_done.wait(dve, q, -2 * JB * (RQ - 1))
                src = misc[ODD:KR, :].rearrange("p (g i two) -> p g i two", g=4, two=2)[:, :, :, 1]
                dst = qr[ODD:KR, c % RQ, :].rearrange("p (i two h) -> p h i two", two=2, h=H)
                dve.tensor_copy(dst[:, 4 * k:4 * k + 4, :, 1], src).then_inc(odd_done.sem, 1)

            def use_p(it, c, b, k):
                r = (c + 3) // QPB % R2
                if k == 1:
                    q_proj.wait(dve, b, 1)
                    qlo_done.wait(dve, b, 0)
                    qhi_done.wait(dve, b, 1)
                    dve.tensor_scalar(q32[:], misc[:], bq[:, 0:1], None, ALU.add).then_inc(q32_done.sem, 1)
                elif k == 2:
                    khi_done.wait(dve, b, 1)
                    dve.scalar_tensor_tensor(out=k_lo[:, r, :], in0=misc[:], scalar=bk[:, 0:1],
                                             in1=k_hi[:, r, :].bitcast(F32), op0=ALU.add, op1=ALU.subtract).then_inc(klo_done.sem, 1)

            def query_parts(it, c, b):
                r = (c + 3) // QPB % R2
                q32_done.wait(dve, b, 1)
                rows_done.wait(dve, at(it, c + 3), -4 * QPB)
                dve.tensor_copy(q_part[:, r, 0, :], q32[:]).then_inc(split.sem, 1)
                split.wait(dve, b, 1)
                dve.tensor_tensor(rest[:], q32[:], q_part[:, r, 0, :], ALU.subtract).then_inc(split.sem, 1)
                split.wait(dve, b, 2)
                dve.tensor_copy(q_part[:, r, 1, :], rest[:]).then_inc(split.sem, 1)
                split.wait(dve, b, 3)
                dve.tensor_tensor(q_part[:, r, 2, :], rest[:], q_part[:, r, 1, :], ALU.subtract).then_inc(split.sem, 1)
                dve.tensor_scalar(neg[:], q32[:], 0.0, None, ALU.min).then_inc(split.sem, 1)

            def finish_sigma(it, c, b):
                r = (c + 3) // QPB % R2
                neg_exp.wait(dve, b, 1)
                g_prod.wait(dve, at(it, c + 3), -QPB)
                dve.scalar_tensor_tensor(out=sigma[:, r, :], in0=q32[:], scalar=0.0, in1=eneg[:], op0=ALU.max,
                                         op1=ALU.add).then_inc(split.sem, 1)

            def use_e(it, c, k):
                q = at(it, c)
                turned = misc[:].rearrange("p (h e) -> p h e", e=32)
                by_head = lambda x: x[:].rearrange("p (h e) -> p h e", h=H)
                spreadh = lambda x: x[:].broadcast_to([P, H, HD])
                if k == 0:
                    o_turned.wait(dve, q, 1)
                    g_step.wait(dve, q, 0)
                    dve.reciprocal(rden[:], turned[:, :, HD:HD + 1]).then_inc(o_step.sem, 1)
                    o_step.wait(dve, q, 1)
                    dve.tensor_scalar(rdeng[:], rden[:], gate[:, 2:3], None, ALU.mult).then_inc(o_step.sem, 1)
                    o_step.wait(dve, q, 2)
                    dve.tensor_tensor(by_head(local), turned[:, :, 0:HD], spreadh(rdeng), ALU.mult).then_inc(o_step.sem, 1)
                elif k == 1:
                    g_prod.wait(dve, q, 1)
                    dve.tensor_scalar(gden[:], misc[:, D:D + H], 1e-6, None, ALU.add).then_inc(g_step.sem, 1)
                    g_step.wait(dve, q, 1)
                    dve.reciprocal(grden[:], gden[:]).then_inc(g_step.sem, 1)
                    g_step.wait(dve, q, 2)
                    dve.tensor_scalar(grdeng[:], grden[:], gate[:, 3:4], None, ALU.mult).then_inc(g_step.sem, 1)
                    g_step.wait(dve, q, 3)
                    dve.tensor_tensor(by_head(glob), misc[:, 0:D].rearrange("p (h e) -> p h e", h=H), spreadh(grdeng),
                                      ALU.mult).then_inc(g_step.sem, 1)
                    g_step.wait(dve, q, 4)
                    mixed_turned.wait(dve, q, 0)
                    dve.tensor_tensor(mixed[:], local[:], glob[:], ALU.add).then_inc(g_step.sem, 1)
                elif k == 3:
                    row = X[:, bass.ds(q, 1), :].rearrange("p a d -> p (a d)")
                    y_prod.wait(dve, q, 1)
                    dve.tensor_tensor(y[:], misc[:, 0:D], row, ALU.add).then_inc(y_done.sem, 1)
                    y_done.wait(dve, q, 1)
                    dve.tensor_scalar(row, y[:], 0.0, None, ALU.add)
                    dve.bn_stats(STATS[:, bass.ds(q, 1), :].rearrange("p a d -> p (a d)"), y[:])

            def maximum(it, c, o):
                q = at(it, c)
                s_done.wait(dve, q, o + 1)
                if o == 0:
                    nm_step.wait(dve, q, 0)
                dve.tensor_reduce(nm[:, o:o + 1], ps_s[:, o % 2, :], AX.X, ALU.max, negate=True).then_inc(max_done.sem, 1)

            def one(it, c):
                b = projected(it, c)
                if b is not None:
                    xT_turned.wait(dve, b, 0)
                    for t in range(QPB):
                        row = at(it, c + 3 + t)
                        ins = dve.tensor_scalar(xn[:, t, :], X[:, bass.ds(row, 1), :].rearrange("p a d -> p (a d)"),
                                                mean[:, bass.ds(row, 1), :].rearrange("p a d -> p (a d)"),
                                                rstd[:, bass.ds(row, 1), :].rearrange("p a d -> p (a d)"),
                                                ALU.subtract, ALU.mult)
                    ins.then_inc(xn_done.sem, 1)
                q = at(it, c - 2)
                if q is not None:
                    pv_done.wait(dve, q, 1)
                    o_turned.wait(dve, q, 0)
                    dve.tensor_copy(oc[:], ps_v[:]).then_inc(oc_done.sem, 1)
                for j in range(2 * JB):
                    for half in range(2):
                        for kind, k, slot, h in USES:
                            if (slot, h) != (j, half) or not present(it, c, kind):
                                continue
                            if kind == "A":
                                use_a(it, c + 2, k)
                            elif kind == "P":
                                use_p(it, c, b, k)
                            elif kind == "E":
                                use_e(it, c - 2, k)
                            else:
                                q = at(it, c + 1)
                                nm_turned.wait(dve, q, 1)
                                nm_in.wait(dve, q, 0)
                                dve.tensor_copy(nmT[:], miscb[0:2 * NO, 0:P]).then_inc(nmT_done.sem, 1)
                        q = at(it, c + 1)
                        if j < 4 and q is not None:
                            for o in (4 * j + 2 * half, 4 * j + 2 * half + 1):
                                maximum(it, c + 1, o)
                    q = at(it, c + 1)
                    if j == 4 and q is not None:
                        max_done.wait(dve, q, NO)
                        nm_turned.wait(dve, q, 0)
                        dve.tensor_copy(nm_part[:, 0, :], nm[:]).then_inc(nm_step.sem, 1)
                        nm_step.wait(dve, q, 1)
                        dve.tensor_tensor(nm_part[:, 1, :], nm[:], nm_part[:, 0, :], ALU.subtract).then_inc(nm_step.sem, 1)
                    if b is not None and j == 5:
                        query_parts(it, c, b)
                    if b is not None and j == 7:
                        finish_sigma(it, c, b)
            run(dve, one)


def load_phase(nc, io, X, STATS):
    D = X.shape[2]
    ROWS = X.shape[1]
    PIECE = 4
    with ExitStack() as ctx:
        NQ = ROWS // PIECE
        x_in = [ctx.enter_context(nc.semaphore(f"x_in{k}")) for k in range(NQ)]
        block = ctx.enter_context(nc.Block())

        @block.sync
        def _(sp):
            for i in range(ROWS // PIECE):
                sp.dma_start(X[:, i * PIECE:(i + 1) * PIECE, :], io["x"][:, i * PIECE:(i + 1) * PIECE, :]).then_inc(x_in[i % NQ], 16)

        @block.vector
        def _(dve):
            for i in range(ROWS // PIECE):
                dve.wait_ge(x_in[i % NQ], 16 * (i // NQ + 1))
                for t in range(PIECE):
                    dve.bn_stats(STATS[:, i * PIECE + t, :], X[:, i * PIECE + t, :])


def macaron_layer(nc, io, out):
    D = io["x"].shape[2]
    ROWS = io["x"].shape[1]
    with ExitStack() as ctx:
        X = ctx.enter_context(nc.sbuf_tensor("X", [P, ROWS, D], F32))
        STATS = ctx.enter_context(nc.sbuf_tensor("STATS", [P, ROWS, 6], F32))
        load_phase(nc, io, X, STATS)
        ffn_phase(nc, io, X, STATS, "ffn1", None)
        attention_phase(nc, io, X, STATS)
        ffn_phase(nc, io, X, STATS, "ffn2", out)


def _shape_constants():
    import numpy as _np

    heads, hd, odd = 16, 8, 64
    pairs = ((1, 1), (1, 2), (2, 1), (2, 2), (1, 3), (3, 1))
    head_of = _np.kron(_np.eye(heads), _np.ones((hd, 1))).astype(_np.float32)
    spread = _np.zeros((128, 3, odd + len(pairs) * hd), _np.float32)
    emb_part = _np.zeros((128, 4), _np.float32)
    for parity in range(2):
        for n, (q_part, e_part) in enumerate(pairs):
            for d in range(hd):
                row = odd * parity + hd * n + d
                spread[d::hd, q_part - 1, row] = 1.0
                emb_part[row, e_part - 1] = 1.0
    emb_part[odd + len(pairs) * hd:odd + len(pairs) * hd + 2, 3] = 1.0
    return {"head_of": head_of, "spread": spread, "emb_part": emb_part}


def kernel(**inputs):
    import numpy as _np
    import concourse.bacc as _bacc
    from concourse import mybir as _mybir
    from concourse.bass_utils import run_bass_kernel_spmd as _run

    nc = _bacc.Bacc("TRN2", target_bir_lowering=False, num_devices=1)
    x = _np.asarray(inputs["L0_attn_hidden_states"])
    f, a = "L0_ffn_", "L0_attn_"
    host = {
        "x": x.reshape(-1, 128, x.shape[-1]),
        "router": inputs[f + "router_DE"],
        "w_in": inputs[f + "w_in_eDF"],
        "w_gate": inputs[f + "w_swiglu_eDF"],
        "w_out": inputs[f + "w_out_eFD"],
        "w_in_s": _np.asarray(inputs[f + "w_in_shared_FD"]).T,
        "w_gate_s": _np.asarray(inputs[f + "w_swiglu_FD"]).T,
        "w_out_s": _np.asarray(inputs[f + "w_out_shared_DF"]).T,
        "ident": _np.eye(128, dtype=_np.float32),
        "wq": _np.asarray(inputs[a + "Wq"]).T,
        "wk": _np.asarray(inputs[a + "Wk"]).T,
        "wv": _np.asarray(inputs[a + "Wv"]).T,
        "wo": _np.asarray(inputs[a + "Wo"]).T,
        "bq": _np.asarray(inputs[a + "bq"]).reshape(128, 1),
        "bk": _np.asarray(inputs[a + "bk"]).reshape(128, 1),
        "bv": _np.asarray(inputs[a + "bv"]).reshape(1, 128),
        "bo": _np.asarray(inputs[a + "bo"]).reshape(1, 128),
        "M": inputs[a + "M"],
        "z": _np.asarray(inputs[a + "z"]).reshape(128, 1),
        "alpha": _np.asarray(inputs[a + "gate_alpha"]).reshape(1, 1),
        "rel": _np.asarray(inputs[a + "rel_emb"])[::-1].T,
        **_shape_constants(),
        "ranks": _np.tile(_np.arange(8, 0, -1, dtype=_np.float32), (128, 4, 1)),
    }
    arrays, io = {}, {}
    for name, a in host.items():
        a = _np.ascontiguousarray(a)
        arrays["in_" + name] = a
        io[name] = nc.dram_tensor("in_" + name, a.shape, _mybir.dt.from_np(a.dtype), kind="ExternalInput").ap()
    io["alpha"] = io["alpha"].broadcast_to([128, 1])
    io["x"] = io["x"].rearrange("r p d -> p r d")
    out = nc.dram_tensor("out_0", x.shape, _mybir.dt.float32, kind="ExternalOutput").ap()
    macaron_layer(nc, io, out.rearrange("b (r p) d -> p (b r) d", p=128))
    r = _run(nc, [arrays], core_ids=[0])
    return r.results[0]["out_0"]
```

```python
from contextlib import ExitStack

import concourse.bass as bass
from concourse import mybir

P = 128
F32, F32R, BF16, U32 = mybir.dt.float32, mybir.dt.float32r, mybir.dt.bfloat16, mybir.dt.uint32
ALU, ACT, AX = mybir.AluOpType, mybir.ActivationFunctionType, mybir.AxisListType
EPS = 1e-5


class Ring:

    def __init__(self, sem, per):
        self.sem, self.per = sem, per

    def wait(self, eng, n, c):
        if isinstance(n, int) and n * self.per + c <= 0:
            return
        eng.wait_ge(self.sem, n * self.per + c)


def mean_and_variance(dve, STATS, work, done):
    D = P
    STEPS = (
        lambda: dve.tensor_tensor(work[0], STATS[:, :, 1:2], STATS[:, :, 4:5], ALU.add),
        lambda: dve.tensor_tensor(work[1], STATS[:, :, 1:2], STATS[:, :, 4:5], ALU.subtract),
        lambda: dve.tensor_scalar(work[2], work[0], 0.5, None, ALU.mult),
        lambda: dve.tensor_scalar(work[3], work[1], 0.5, None, ALU.mult),
        lambda: dve.tensor_tensor(work[4], work[3], work[3], ALU.mult),
        lambda: dve.tensor_tensor(work[5], STATS[:, :, 2:3], STATS[:, :, 5:6], ALU.add),
        lambda: dve.scalar_tensor_tensor(out=work[6], in0=work[5], scalar=1.0 / D, in1=work[4], op0=ALU.mult, op1=ALU.add),
    )
    for i, step in enumerate(STEPS):
        step().then_inc(done.sem, 1)
        dve.wait_ge(done.sem, i + 1)


def ffn_phase(nc, io, X, STATS, tag, store):
    D, E, F = P, io["router"].shape[1], io["w_in"].shape[2]
    NE, C = E + 1, F // P
    U = NE * C
    T = 4
    N = X.shape[1] // T
    W = T * P
    R = 2
    RH = 6
    RE = 4
    RAW = 8
    DELAY = 4
    NEXT = U - 8
    SCALED = {0: 2, 1: 3, 2: 4, 3: 5, 4: 6, 5: 7, 6: 8}
    GATED = {NEXT + 4: (0,), NEXT + 5: (1,), NEXT + 6: (2, 3)}
    LOW = 3
    assert E % R == 0 and U % RH == 0 and U % 2 == 0 and E % RE == 0

    with ExitStack() as ctx:
        def sb(name, shape, dt):
            return ctx.enter_context(nc.sbuf_tensor(f"{tag}_{name}", shape, dt))

        def ps(name, shape, dt=F32):
            return ctx.enter_context(nc.psum_tensor(f"{tag}_{name}", shape, dt))

        def ring(name, per):
            return Ring(ctx.enter_context(nc.semaphore(f"{tag}_{name}")), per)

        raw = sb("raw", [P, RAW, max(C * D, F)], F32)
        w_mid = sb("w_mid", [P, 2, NE, F], F32R)
        w_gate = sb("w_gate", [P, 2, NE, F], F32R)
        w_out = sb("w_out", [P, 2, NE, C, D], F32R)
        router32 = sb("router32", [P, E], F32)
        router = sb("router", [P, 2, E], F32R)
        partial = sb("partial", [P, W], F32)
        ident = sb("ident", [P, P], F32)
        ranks_sb = sb("ranks_sb", [P, T, E], F32)
        ranks = ranks_sb[:]
        rstd = sb("rstd", [P, N * T, 1], F32)
        std = sb("std", [P, N * T, 1], F32)
        eps, warm = sb("eps", [P, 1], F32), sb("warm", [P, 1], F32)
        moments = sb("moments", [P, 7, N * T, 1], F32)
        mean, var = moments[:, 2], moments[:, 6]
        xn = sb("xn", [P, T, D], F32)
        xe = sb("xe", [P, RE, T, D], F32)
        xT_hi = sb("xT_hi", [P, R + 1, W], F32R)
        xT_lo = sb("xT_lo", [P, R + 1, W], F32R)
        silu = sb("silu", [P, RH, W], F32)
        h = sb("h", [P, RH, W], F32)
        h_hi = sb("h_hi", [P, RH, W], F32R)
        h_lo = sb("h_lo", [P, RH, W], F32R)
        scores = sb("scores", [P, T, E], F32)
        tanh = sb("tanh", [P, T, E], F32)
        top = sb("top", [P, 2, T, 1], F32)
        lead = sb("lead", [P, T, 1], F32)
        rest = sb("rest", [P, T, E], F32)
        order = sb("order", [P, T, E], F32)
        pick = sb("pick", [P, 2, T, E], F32)
        gate = sb("gate", [P, T, E], F32)
        oT = sb("oT", [P, W], F32)
        y = sb("y", [P, T, D], F32)

        ps_x = ps("ps_x", [P, 2, W])
        ps_mid = ps("ps_mid", [P, 2, W])
        ps_gate = ps("ps_gate", [P, 2, W])
        ps_out = ps("ps_out", [P, W])
        ps_misc = ps("ps_misc", [P, W])

        const_in = ring("const_in", 0)
        raw_in = [ring(f"raw_in{k}", 0) for k in range(RAW)]
        w_hi = ring("w_hi", 0)
        split = ring("split", 0)
        consts = ring("consts", 0)
        stats_done = ring("stats_done", 0)
        sqrt_done = ring("sqrt_done", 0)
        rstd_done = ring("rstd_done", 0)
        xn_done = ring("xn_done", 1)
        x0_turned = ring("x0_turned", 1)
        x0hi_done = ring("x0hi_done", 1)
        x0lo_done = ring("x0lo_done", 1)
        xT_done = ring("xT_done", E)
        xhi_done = ring("xhi_done", E)
        xlo_done = ring("xlo_done", E)
        part_scored = ring("part_scored", 1)
        part_out = ring("part_out", 1)
        routed = ring("routed", 1)
        tanh_done = ring("tanh_done", 1)
        chain = ring("chain", 16)
        xe_done = ring("xe_done", E)
        mid_done = ring("mid_done", U)
        silu_done = ring("silu_done", U)
        h_done = ring("h_done", U)
        hhi_done = ring("hhi_done", U)
        hlo_pool = ring("hlo_pool", U - U // LOW)
        hlo_dve = ring("hlo_dve", U // LOW)
        out_done = ring("out_done", U)
        oT_done = ring("oT_done", 1)
        turned = ring("turned", 1)
        y_done = ring("y_done", 2)
        stored = ring("stored", 16)

        def low_wait(eng, n, u):
            v, n = (u, n) if u >= 0 else (u + U, n - 1)
            if v % LOW == LOW - 1:
                hlo_dve.wait(eng, n, v // LOW + 1)
            else:
                hlo_pool.wait(eng, n, v - v // LOW + 1)

        block = ctx.enter_context(nc.Block())

        weights = [(io["w_in_s"], w_mid[:, :, 0, :]), (io["w_gate_s"], w_gate[:, :, 0, :]),
                   (io["w_out_s"].rearrange("(c p) d -> p c d", p=P), w_out[:, :, 0])]
        for e in range(E):
            weights += [(io["w_in"][e], w_mid[:, :, e + 1, :]), (io["w_gate"][e], w_gate[:, :, e + 1, :]),
                        (io["w_out"][e].rearrange("(c p) d -> p c d", p=P), w_out[:, :, e + 1])]

        def weights_in(u):
            return [i for i in range(3 + 3 * u // 2 + u % 2, 3 + 3 * (u + 1) // 2 + (u + 1) % 2) if i < len(weights)]

        def shaped(ap, to):
            return ap.rearrange("p (c d) -> p c d", c=C) if len(to.shape) == 4 else ap

        @block.sync
        def _(sp):
            for i, (src, to) in enumerate(weights):
                if i == 3:
                    for to_const, const in ((ident[:], "ident"), (router32[:], "router"), (ranks, "ranks")):
                        sp.dma_start(to_const, io[const]).then_inc(const_in.sem, 16)
                if i >= RAW:
                    sp.wait_ge(split.sem, i - RAW + 1)
                sp.dma_start(shaped(raw[:, i % RAW, :], to), src).then_inc(raw_in[i % RAW].sem, 16)
            if store is not None:
                with sp.Fori(0, N) as n:
                    y_done.wait(sp, n, 2)
                    sp.dma_start(store[:, bass.ts(n, T), :], X[:, bass.ts(n, T), :]).then_inc(stored.sem, 16)
                sp.wait_ge(stored.sem, 16 * N)

        @block.tensor
        def _(pe):
            def product(out, lhs, rhs, start, stop):
                for i, (a, b) in enumerate(((0, 0), (0, 1), (1, 0))):
                    ins = pe.matmul(out, lhs(a), rhs(b), start=start and i == 0, stop=stop and i == 2)
                return ins

            def turn_unscaled(n):
                xn_done.wait(pe, n, 1)
                y_done.wait(pe, n, -3)
                for t in range(T):
                    ins = pe.transpose(ps_misc[:, t * P:(t + 1) * P], xn[:, t, :], ident[:])
                ins.then_inc(x0_turned.sem, 1)

            def turn_in(n, e):
                xe_done.wait(pe, n, e)
                xlo_done.wait(pe, n, e - 2)
                for t in range(T):
                    ins = pe.transpose(ps_x[:, e % 2, t * P:(t + 1) * P], xe[:, e % RE, t, :], ident[:])
                ins.then_inc(xT_done.sem, 1)

            def route(n):
                x0lo_done.wait(pe, n, 1)
                parts = router[:].rearrange("p a e -> p (a e)")
                for i, x in enumerate((xT_hi, xT_lo)):
                    ins = pe.matmul(ps_misc[0:2 * E, :], parts, x[:, R, :], start=(i == 0), stop=(i == 1))
                ins.then_inc(part_scored.sem, 1)

            def turn_scores(n):
                part_out.wait(pe, n, 1)
                for t in range(T):
                    ins = pe.transpose(ps_misc[:, t * P:(t + 1) * P], partial[:, t * P:(t + 1) * P], ident[:])
                ins.then_inc(routed.sem, 1)

            def unit(n, u):
                e, c = divmod(u, C)
                if e == 0:
                    x0lo_done.wait(pe, n, 1)
                else:
                    xlo_done.wait(pe, n, e)
                h_done.wait(pe, n, u - 1)
                for w, dst in ((w_mid, ps_mid), (w_gate, ps_gate)):
                    ins = product(dst[:, u % 2, :], lambda a: w[:, a, e, c * P:(c + 1) * P],
                                  lambda b: (xT_hi, xT_lo)[b][:, e % R if e else R, :], True, True)
                ins.then_inc(mid_done.sem, 1)

            def output(n, u):
                e, c = divmod(u, C)
                hhi_done.wait(pe, n, u + 1)
                low_wait(pe, n, u)
                if u == 0:
                    oT_done.wait(pe, n, 0)
                product(ps_out[:], lambda a: w_out[:, a, e, c, :], lambda b: (h_hi, h_lo)[b][:, u % RH, :],
                        u == 0, u == U - 1).then_inc(out_done.sem, 1)

            def turn_out(n):
                oT_done.wait(pe, n, 1)
                chain.wait(pe, n + 1, 2) if n_has_next(n) else None
                for t in range(T):
                    ins = pe.transpose(ps_misc[:, t * P:(t + 1) * P], oT[:, t * P:(t + 1) * P], ident[:])
                ins.then_inc(turned.sem, 1)

            def tile(n, first, last):
                for u in range(U):
                    e, c = divmod(u, C)
                    if u == DELAY + 1 and not first:
                        turn_out(n - 1)
                    if c == 0 and 0 < e < NE - 1 or u == 1:
                        turn_in(n, e + 1)
                    if u == NEXT and not last:
                        turn_unscaled(n + 1)
                    if u == NEXT + 2 and not last:
                        route(n + 1)
                    if u == NEXT + 4 and not last:
                        turn_scores(n + 1)
                    if first:
                        pe.wait_ge(split.sem, 3 * (e + 1))
                    unit(n, u)
                    if u >= DELAY:
                        output(n, u - DELAY)
                    elif not first:
                        output(n - 1, u - DELAY + U)

            def n_has_next(n):
                return not (isinstance(n, int) and n == N - 1)

            pe.wait_ge(const_in.sem, 48)
            turn_unscaled(0)
            pe.wait_ge(consts.sem, 3)
            route(0)
            turn_scores(0)
            tile(0, True, False)
            with pe.Fori(1, N - 1) as n:
                tile(n, False, False)
            tile(N - 1, False, True)
            for u in range(U - DELAY, U):
                output(N - 1, u)
            turn_out(N - 1)

        @block.scalar
        def _(act):
            def unscaled_high(n):
                x0_turned.wait(act, n, 1)
                mid_done.wait(act, n - 1, C)
                act.copy(xT_hi[:, R, :], ps_misc[:]).then_inc(x0hi_done.sem, 1)

            def x_high(n, e):
                xT_done.wait(act, n, e)
                mid_done.wait(act, n, C * (e - 1))
                act.copy(xT_hi[:, e % R, :], ps_x[:, e % 2, :]).then_inc(xhi_done.sem, 1)

            def h_high(n, u):
                h_done.wait(act, n, u + 1)
                out_done.wait(act, n, u - RH + 1)
                act.copy(h_hi[:, u % RH, :], h[:, u % RH, :]).then_inc(hhi_done.sem, 1)

            def leave(n):
                out_done.wait(act, n, U)
                turned.wait(act, n, 0)
                act.copy(oT[:], ps_out[:]).then_inc(oT_done.sem, 1)

            def partial_out(n):
                part_scored.wait(act, n, 1)
                routed.wait(act, n, 0)
                act.copy(partial[0:2 * E, :], ps_misc[0:2 * E, :]).then_inc(part_out.sem, 1)

            def gates(n):
                chain.wait(act, n, 2)
                act.activation(tanh[:], scores[:], ACT.Tanh, scale=0.5).then_inc(tanh_done.sem, 1)

            def weight_high(i):
                to = weights[i][1]
                act.wait_ge(raw_in[i % RAW].sem, 16 * (i // RAW + 1))
                act.copy(to[:, 0], shaped(raw[:, i % RAW, :], to)).then_inc(w_hi.sem, 1)

            def tile(n, first, last):
                for u in range(U):
                    e, c = divmod(u, C)
                    if first:
                        for i in weights_in(u):
                            weight_high(i)
                    if u == DELAY and not first:
                        leave(n - 1)
                    if c == 0 and 0 < e < NE - 1 or u == 1:
                        x_high(n, e + 1)
                    if u == NEXT and not last:
                        unscaled_high(n + 1)
                    if u == NEXT + 3 and not last:
                        partial_out(n + 1)
                    if u == NEXT + 6 and not last:
                        gates(n + 1)
                    if u > 0:
                        h_high(n, u - 1)
                    elif not first:
                        h_high(n - 1, U - 1)
                    mid_done.wait(act, n, u + 1)
                    h_done.wait(act, n, u - RH + 1)
                    act.activation(silu[:, u % RH, :], ps_mid[:, u % 2, :], ACT.Silu).then_inc(silu_done.sem, 1)

            act.wait_ge(consts.sem, 1)
            act.activation(warm[:], eps[:], ACT.Sqrt)
            act.wait_ge(stats_done.sem, 7)
            act.activation(std[:], var, ACT.Sqrt, bias=eps[:, 0:1]).then_inc(sqrt_done.sem, 1)
            for i in range(3):
                weight_high(i)
            unscaled_high(0)
            partial_out(0)
            gates(0)
            tile(0, True, False)
            with act.Fori(1, N - 1) as n:
                tile(n, False, False)
            tile(N - 1, False, True)
            h_high(N - 1, U - 1)
            leave(N - 1)

        @block.gpsimd
        def _(pool):
            def scale(n, e):
                chain.wait(pool, n, 16)
                xT_done.wait(pool, n, e - RE + 1)
                pool.tensor_tensor(xe[:, e % RE], xn[:], gate[:, :, e - 1:e].broadcast_to([P, T, D]),
                                   ALU.mult).then_inc(xe_done.sem, 1)

            def h_low(n, u):
                hhi_done.wait(pool, n, u + 1)
                out_done.wait(pool, n, u - RH + 1)
                pool.tensor_tensor(h_lo[:, u % RH, :], h[:, u % RH, :], h_hi[:, u % RH, :].bitcast(F32),
                                   ALU.subtract).then_inc(hlo_pool.sem, 1)

            def tile(n, first, last):
                for u in range(U):
                    if u == U - 1 and not last:
                        scale(n + 1, 1)
                    if u % LOW:
                        h_low(n, u - 1)
                    if u in SCALED:
                        scale(n, SCALED[u])

            scale(0, 1)
            tile(0, True, False)
            with pool.Fori(1, N - 1) as n:
                tile(n, False, False)
            tile(N - 1, False, True)

        @block.vector
        def _(dve):
            def normalise(n):
                xe_done.wait(dve, n, 0)
                for t in range(T):
                    r = n * T + t
                    ins = dve.tensor_scalar(xn[:, t, :], X[:, bass.ds(r, 1), :].rearrange("p a d -> p (a d)"),
                                            mean[:, bass.ds(r, 1), :].rearrange("p a d -> p (a d)"),
                                            rstd[:, bass.ds(r, 1), :].rearrange("p a d -> p (a d)"),
                                            ALU.subtract, ALU.mult)
                ins.then_inc(xn_done.sem, 1)

            def unscaled_low(n):
                x0hi_done.wait(dve, n, 1)
                dve.tensor_tensor(xT_lo[:, R, :], ps_misc[:], xT_hi[:, R, :].bitcast(F32),
                                  ALU.subtract).then_inc(x0lo_done.sem, 1)

            def x_low(n, e):
                xhi_done.wait(dve, n, e)
                dve.tensor_tensor(xT_lo[:, e % R, :], ps_x[:, e % 2, :], xT_hi[:, e % R, :].bitcast(F32),
                                  ALU.subtract).then_inc(xlo_done.sem, 1)

            def gates(n, part):
                k, half = divmod(part, 2)
                left = (scores, rest)[k]
                c = 2 + 6 * k
                if part == 0:
                    routed.wait(dve, n, 1)
                    xe_done.wait(dve, n, 0)
                    by_part = ps_misc[:].rearrange("p (t a e) -> p t a e", t=T, e=E)
                    dve.tensor_copy(scores[:], by_part[:, :, 0]).then_inc(chain.sem, 1)
                    chain.wait(dve, n, 1)
                    dve.tensor_tensor(scores[:], scores[:], by_part[:, :, 1], ALU.add).then_inc(chain.sem, 1)
                if half == 0:
                    chain.wait(dve, n, c)
                    dve.tensor_reduce(top[:, k], left[:], AX.X, ALU.max).then_inc(chain.sem, 1)
                    chain.wait(dve, n, c + 1)
                    dve.tensor_tensor(pick[:, k], left[:], top[:, k].broadcast_to([P, T, E]), ALU.is_equal).then_inc(chain.sem, 1)
                    chain.wait(dve, n, c + 2)
                    dve.tensor_tensor(order[:], pick[:, k], ranks, ALU.mult).then_inc(chain.sem, 1)
                    return
                chain.wait(dve, n, c + 3)
                dve.tensor_reduce(lead[:], order[:], AX.X, ALU.max).then_inc(chain.sem, 1)
                chain.wait(dve, n, c + 4)
                dve.tensor_tensor(pick[:, k], ranks, lead[:].broadcast_to([P, T, E]), ALU.is_equal).then_inc(chain.sem, 1)
                chain.wait(dve, n, c + 5)
                if k == 0:
                    dve.scalar_tensor_tensor(out=rest[:], in0=pick[:, 0], scalar=-3e38, in1=scores[:],
                                             op0=ALU.mult, op1=ALU.add).then_inc(chain.sem, 1)
                else:
                    dve.tensor_tensor(order[:], pick[:, 0], pick[:, 1], ALU.add).then_inc(chain.sem, 1)
                    tanh_done.wait(dve, n, 1)
                    dve.tensor_scalar(tanh[:], tanh[:], 0.5, 0.5, ALU.mult, ALU.add).then_inc(chain.sem, 1)
                    chain.wait(dve, n, 15)
                    dve.tensor_tensor(gate[:], tanh[:], order[:], ALU.mult).then_inc(chain.sem, 1)

            def h_low(n, u):
                hhi_done.wait(dve, n, u + 1)
                out_done.wait(dve, n, u - RH + 1)
                dve.tensor_tensor(h_lo[:, u % RH, :], h[:, u % RH, :], h_hi[:, u % RH, :].bitcast(F32),
                                  ALU.subtract).then_inc(hlo_dve.sem, 1)

            def residual(n):
                turned.wait(dve, n, 1)
                rows = X[:, bass.ds(n * T, T), :].rearrange("p t d -> p (t d)")
                flat = y[:].rearrange("p t d -> p (t d)")
                dve.scalar_tensor_tensor(out=flat, in0=ps_misc[:], scalar=0.5, in1=rows, op0=ALU.mult,
                                         op1=ALU.add).then_inc(y_done.sem, 1)
                y_done.wait(dve, n, 1)
                dve.tensor_scalar(rows, flat, 0.0, None, ALU.add).then_inc(y_done.sem, 1)
                for t in range(T):
                    dve.bn_stats(STATS[:, bass.ds(n * T + t, 1), :].rearrange("p a d -> p (a d)"), y[:, t, :])

            def weight_low(i):
                to = weights[i][1]
                dve.wait_ge(w_hi.sem, i + 1)
                dve.tensor_tensor(to[:, 1], shaped(raw[:, i % RAW, :], to), to[:, 0].bitcast(F32),
                                  ALU.subtract).then_inc(split.sem, 1)

            def tile(n, first, last):
                for u in range(U):
                    e, c = divmod(u, C)
                    if first:
                        for i in weights_in(u):
                            weight_low(i)
                    if c == 0 and 0 < e < NE - 1 or u == 1:
                        x_low(n, e + 1)
                    if u == NEXT and not last:
                        unscaled_low(n + 1)
                    silu_done.wait(dve, n, u + 1)
                    hhi_done.wait(dve, n, u - RH + 1)
                    low_wait(dve, n, u - RH)
                    dve.tensor_tensor(h[:, u % RH, :], silu[:, u % RH, :], ps_gate[:, u % 2, :],
                                      ALU.mult).then_inc(h_done.sem, 1)
                    if u % LOW == 0 and (u > 0 or not first):
                        h_low(*((n, u - 1) if u > 0 else (n - 1, U - 1)))
                    if u == DELAY + 2 and not first:
                        residual(n - 1)
                    if u == NEXT - 3 and not last:
                        normalise(n + 1)
                    if u in GATED and not last:
                        for part in GATED[u]:
                            gates(n + 1, part)

            dve.memset(partial[:], 0.0)
            dve.memset(eps[:], EPS).then_inc(consts.sem, 1)
            mean_and_variance(dve, STATS, [moments[:, i] for i in range(7)], stats_done)
            dve.wait_ge(sqrt_done.sem, 1)
            dve.reciprocal(rstd[:], std[:]).then_inc(rstd_done.sem, 1)
            dve.wait_ge(rstd_done.sem, 1)
            normalise(0)
            dve.wait_ge(const_in.sem, 48)
            for b in range(2):
                if b == 0:
                    dve.tensor_copy(router[:, 0, :], router32[:]).then_inc(consts.sem, 1)
                else:
                    dve.wait_ge(consts.sem, 2)
                    dve.tensor_tensor(router[:, 1, :], router32[:], router[:, 0, :].bitcast(F32), ALU.subtract).then_inc(consts.sem, 1)
            for i in range(3):
                weight_low(i)
            unscaled_low(0)
            for part in range(4):
                gates(0, part)
            tile(0, True, False)
            with dve.Fori(1, N - 1) as n:
                tile(n, False, False)
            tile(N - 1, False, True)
            h_low(N - 1, U - 1)
            residual(N - 1)


def attention_phase(nc, io, X, STATS):
    D = X.shape[2]
    H, HD = io["M"].shape[0], io["M"].shape[1]
    Q = X.shape[1]
    QPB = 4
    S = QPB * P
    B = Q // QPB
    COLS = P * H
    REL = (io["rel"].shape[1] - 1) // 2
    SCALE = float(HD) ** -0.5
    OCT = P // H
    NO = P // OCT
    JB = 4
    IB = P // JB
    RS, RT = 4, 2
    LAG = 2
    BANDS = (((1, 1), (1, 2), (1, 3)), ((2, 1), (2, 2), (3, 1)))
    ODD = 64
    PARTS_OF = ((0,), (1, 2))
    WIN = 2 * S
    NREL = 2 * REL + 1
    HALF = S // 2
    VW = H * (HD + 1) + 32 - (HD + 1) + 1
    R2 = 2
    HA = 512 // (P // 2)
    UNROLL = 8

    with ExitStack() as ctx:
        def sb(name, shape, dt=F32):
            return ctx.enter_context(nc.sbuf_tensor(f"at_{name}", shape, dt))

        def ps(name, shape, dt=F32):
            return ctx.enter_context(nc.psum_tensor(f"at_{name}", shape, dt))

        def ring(name, per):
            return Ring(ctx.enter_context(nc.semaphore(f"at_{name}")), per)

        ident = sb("ident", [P, P])
        wq, wk, wv, wo = (sb(w, [P, D]) for w in ("wq", "wk", "wv", "wo"))
        bq, bk = sb("bq", [P, 1]), sb("bk", [P, 1])
        bk_far = sb("bk_far", [P, 2])
        bv, bo, ones = sb("bv", [1, D]), sb("bo", [1, D]), sb("ones", [1, P])
        head_of = sb("head_of", [P, H])
        spread = sb("spread", [P, 3, P], BF16)
        pick = sb("pick", [P, H, 3, P], BF16)
        emb_part = sb("emb_part", [P, 3])
        rel_part = sb("rel_part", [P, 3, NREL], BF16)
        window = sb("window", [P, WIN], BF16)
        mz = sb("mz", [P, D + H])
        m_sb, z_sb = sb("m_sb", [P, HD]), sb("z_sb", [P, 1])
        gate = sb("gate", [P, 4])
        gate1 = sb("gate1", [P, 1])
        eps, warm = sb("eps", [P, 1]), sb("warm", [P, 1])
        moments = sb("moments", [P, 7, Q, 1])
        mean, var = moments[:, 2], moments[:, 6]
        std, rstd = sb("std", [P, Q, 1]), sb("rstd", [P, Q, 1])
        xn = sb("xn", [P, QPB, D])
        xT = sb("xT", [P, S])
        q32 = sb("q32", [P, S])
        rest = sb("rest", [P, S])
        q_hi, q_lo = sb("q_hi", [P, R2, S], F32R), sb("q_lo", [P, R2, S], F32R)
        q_part = sb("q_part", [P, R2, 3, S], BF16)
        k_hi, k_lo = sb("k_hi", [P, R2, S], F32R), sb("k_lo", [P, R2, S], F32R)
        far_hi, far_lo = sb("far_hi", [P, R2, S], F32R), sb("far_lo", [P, R2, S], F32R)
        v = sb("v", [P, R2, QPB, VW])
        neg = sb("neg", [P, S])
        eneg = rest
        sigma = sb("sigma", [P, R2, S])
        qd_hi = sb("qd_hi", [P, P, H], F32R)
        qd_lo = sb("qd_lo", [P, P, H], F32R)
        qr = sb("qr", [P, R2, COLS], BF16)
        nm = sb("nm", [P, NO])
        expo = sb("expo", [P, RS, S])
        probs = sb("probs", [P, R2, QPB, H, P])
        scratch = probs[:, 0, 0].rearrange("p h i -> p (h i)")
        spread32 = scratch[:, P * 9:P * 12].rearrange("p (a r) -> p a r", a=3)
        rel, rel_rest, rel_row = (scratch[:, x * P * 3:x * P * 3 + NREL] for x in range(3))
        oc = sb("oc", [P, 512])
        rden = sb("rden", [P, H, 1])
        rdeng = sb("rdeng", [P, H, 1])
        gden = sb("gden", [P, H, 1])
        grden = sb("grden", [P, H, 1])
        grdeng = sb("grdeng", [P, H, 1])
        local, glob, mixed, mixedT = (sb(x, [P, D]) for x in ("local", "glob", "mixed", "mixedT"))
        y = sb("y", [P, D])

        ps_s = ps("ps_s", [P, RS, S])
        ps_t = ps("ps_t", [P, RT, QPB * P])
        ps_v = ps("ps_v", [P, 512])
        misc = ps("misc", [P, 512])

        const_in, scaled, split_rel, gate_step, step, stats_done, table = (
            ring(x, 0) for x in ("const_in", "scaled", "split_rel", "gate_step", "step", "stats_done", "table"))
        loads = [(rel, io["rel"]), (emb_part[:], io["emb_part"]), (wk[:], io["wk"]), (bk[:], io["bk"]),
                 (head_of[:], io["head_of"]), (spread32, io["spread"]), (z_sb[:], io["z"]),
                 (m_sb[:], io["M"].rearrange("h d v -> (h d) v")), (gate[:, 0:1], io["alpha"]), (ident[:], io["ident"]),
                 (wq[:], io["wq"]), (bq[:], io["bq"]), (wv[:], io["wv"]), (bv[:], io["bv"]), (wo[:], io["wo"]),
                 (bo[:], io["bo"])]
        with nc.Block() as block:
            @block.sync
            def _(sp):
                for to, src in loads[0::2]:
                    sp.dma_start(to, src).then_inc(const_in.sem, 16)

            @block.scalar
            def _(act):
                for to, src in loads[1::2]:
                    act.dma_start(to, src).then_inc(const_in.sem, 16)
                act.wait_ge(table.sem, 1)
                act.activation(warm[:], eps[:], ACT.Sqrt)
                act.wait_ge(stats_done.sem, 7)
                act.activation(std[:], var, ACT.Sqrt, bias=eps[:, 0:1]).then_inc(step.sem, 1)
                act.wait_ge(const_in.sem, 16 * len(loads))
                act.activation(gate[:, 1:2], gate[:, 0:1], ACT.Exp, scale=-1.0).then_inc(step.sem, 1)

            @block.gpsimd
            def _(pool):
                pool.memset(qr[:].rearrange("p r c -> p (r c)").bitcast(U32), 0)
                pool.memset(v[:], 1.0)

            @block.vector
            def _(dve):
                dve.memset(eps[:], EPS).then_inc(table.sem, 1)
                dve.memset(window[:].bitcast(U32), 0)
                dve.memset(ones[:], 1.0)
                mean_and_variance(dve, STATS, [moments[:, i] for i in range(7)], stats_done)
                dve.wait_ge(const_in.sem, 16 * len(loads))
                dve.tensor_scalar(wk[:], wk[:], SCALE, None, ALU.mult)
                dve.tensor_scalar(bk[:], bk[:], SCALE, None, ALU.mult)
                dve.tensor_scalar(rel_rest, rel, SCALE, None, ALU.mult).then_inc(scaled.sem, 1)
                dve.wait_ge(scaled.sem, 1)
                for end in range(2):
                    dve.tensor_tensor(bk_far[:, end:end + 1], bk[:], rel_rest[:, 2 * REL * end:2 * REL * end + 1], ALU.add)
                for i in range(3):
                    dve.tensor_copy(rel_part[:, i], rel_rest).then_inc(split_rel.sem, 1)
                    dve.wait_ge(split_rel.sem, 2 * i + 1)
                    dve.tensor_tensor(rel_rest, rel_rest, rel_part[:, i], ALU.subtract).then_inc(split_rel.sem, 1)
                    dve.wait_ge(split_rel.sem, 2 * i + 2)
                dve.tensor_scalar(rel_row, rel_part[:, 0], emb_part[:, 0:1], None, ALU.mult).then_inc(table.sem, 1)
                for i in (1, 2):
                    dve.wait_ge(table.sem, i + 1)
                    dve.scalar_tensor_tensor(out=rel_row, in0=rel_part[:, i], scalar=emb_part[:, i:i + 1], in1=rel_row,
                                             op0=ALU.mult, op1=ALU.add).then_inc(table.sem, 1)
                dve.wait_ge(table.sem, 4)
                for par in range(2):
                    rows = slice(ODD * par, ODD * par + ODD)
                    at = S - REL + par
                    dve.tensor_copy(window[rows, at:at + NREL], rel_row[rows, :])
                    dve.tensor_scalar(window[rows, 0:at], window[rows, 0:at], rel_row[rows, 0:1], None, ALU.add)
                    dve.tensor_scalar(window[rows, at + NREL:WIN], window[rows, at + NREL:WIN],
                                      rel_row[rows, NREL - 1:NREL], None, ALU.add)
                dve.tensor_copy(spread[:], spread32).then_inc(table.sem, 1)
                dve.wait_ge(table.sem, 5)
                for h in range(H):
                    dve.tensor_scalar(pick[:, h], spread[:], head_of[:, h:h + 1], None, ALU.mult)
                mzv = mz[:, 0:D].rearrange("p (h v) -> p h v", h=H)
                dve.tensor_tensor(mzv, head_of[:].rearrange("p (h a) -> p h a", a=1).broadcast_to([P, H, HD]),
                                  m_sb[:].rearrange("p (a v) -> p a v", a=1).broadcast_to([P, H, HD]), ALU.mult)
                dve.tensor_scalar(mz[:, D:D + H], head_of[:], z_sb[:, 0:1], None, ALU.mult)
                dve.wait_ge(step.sem, 2)
                dve.reciprocal(rstd[:], std[:])
                dve.tensor_scalar(gate1[:], gate[:, 1:2], 1.0, None, ALU.add).then_inc(gate_step.sem, 1)
                dve.wait_ge(gate_step.sem, 1)
                dve.reciprocal(gate[:, 2:3], gate1[:]).then_inc(gate_step.sem, 1)
                dve.wait_ge(gate_step.sem, 2)
                dve.tensor_scalar(gate[:, 3:4], gate[:, 2:3], -1.0, 1.0, ALU.mult, ALU.add)

        xn_done = ring("xn_done", 1)
        xT_turned = ring("xT_turned", 1)
        xT_done = ring("xT_done", 1)
        q_proj, k_proj, v_proj = (ring(x, 1) for x in ("q_proj", "k_proj", "v_proj"))
        qhi_done = ring("qhi_done", 1)
        q32_done = ring("q32_done", 1)
        qlo_done = ring("qlo_done", 1)
        split = ring("split", 6)
        neg_exp = ring("neg_exp", 1)
        khi_done, klo_done = ring("khi_done", 1), ring("klo_done", 1)
        v_done = ring("v_done", 1)
        rows_done = ring("rows_done", H // HA)
        even_done = ring("even_done", H // HA)
        odd_done = ring("odd_done", H // HA)
        qdhi_done = ring("qdhi_done", JB)
        qdlo_done = ring("qdlo_done", JB)
        s_done = ring("s_done", NO)
        max_done = ring("max_done", NO)
        exp_done = ring("exp_done", NO)
        t_done = ring("t_done", NO)
        tact_done = ring("tact_done", NO // 2)
        tdve_done = ring("tdve_done", NO // 2)
        pv_done = ring("pv_done", 1)
        oc_done = ring("oc_done", 1)
        o_turned = ring("o_turned", 1)
        o_step = ring("o_step", 3)
        g_prod = ring("g_prod", 1)
        g_step = ring("g_step", 5)
        mixed_turned = ring("mixed_turned", 1)
        mixedT_done = ring("mixedT_done", 1)
        y_prod = ring("y_prod", 1)
        y_done = ring("y_done", 1)

        block = ctx.enter_context(nc.Block())

        def run(eng, step_of):
            first, loops = UNROLL - 3, (Q - UNROLL) // UNROLL
            for c in range(-3, first):
                step_of(0, c)
            with eng.Fori(0, loops) as it:
                for c in range(first, first + UNROLL):
                    step_of(it, c)
            for c in range(first + loops * UNROLL, Q + 2):
                step_of(0, c)

        def at(it, c):
            if isinstance(it, int):
                return c if 0 <= c < Q else None
            return it * UNROLL + c

        def seq(it, c):
            return c // QPB if isinstance(it, int) else it * (UNROLL // QPB) + c // QPB

        def projected(it, c):
            if c % QPB != 1 or at(it, c + 3) is None:
                return None
            return seq(it, c + 3)

        USES = [("A", 0, 0), ("E", 0, 2), ("P", 0, 3), ("E", 1, 5), ("P", 1, 7), ("A", 1, 9), ("P", 2, 10),
                ("E", 2, 12), ("P", 3, 13), ("E", 3, 15)]
        VALUES = (4, 5, 7, 8, 10, 11, 13, 14)

        def present(it, c, kind):
            return {"A": at(it, c + 1), "P": projected(it, c), "E": at(it, c - 2)}[kind] is not None

        def uses(it, c, o):
            return [use for use in USES if use[2] == o and present(it, c, use[0])]

        def turned_at(c, o):
            return (c, o - LAG) if o >= LAG else (c - 1, o - LAG + NO)

        def misc_free(pe, it, c, use):
            i = USES.index(use)
            while True:
                i -= 1
                if i < 0:
                    i, c = len(USES) - 1, c - 1
                    if c < -3:
                        return
                kind, k = USES[i][:2]
                if present(it, c, kind):
                    break
            if kind == "A":
                even_done.wait(pe, at(it, c + 1), k + 1)
                odd_done.wait(pe, at(it, c + 1), k + 1)
            elif kind == "E":
                q = at(it, c - 2)
                [lambda: o_step.wait(pe, q, 3), lambda: g_step.wait(pe, q, 4), lambda: mixedT_done.wait(pe, q, 1),
                 lambda: y_done.wait(pe, q, 1)][k]()
            else:
                b = projected(it, c)
                if k == 0:
                    xT_done.wait(pe, b, 1)
                elif k == 1:
                    qhi_done.wait(pe, b, 1)
                    q32_done.wait(pe, b, 1)
                elif k == 2:
                    klo_done.wait(pe, b, 1)
                else:
                    v_done.wait(pe, b, 1)

        @block.tensor
        def _(pe):
            def use_a(it, c, k):
                q, b, r = at(it, c), seq(it, c), c // QPB % R2
                split.wait(pe, b, 6)
                i0 = c % QPB * P
                for g in range(HA):
                    for turn_of in range(2):
                        for band in range(4):
                            parity, parts_of = band // 2, PARTS_OF[band % 2]
                            if turn_of >= len(parts_of):
                                continue
                            part = parts_of[turn_of]
                            rows = slice(32 * band, 32 * band + 32)
                            src = q_part[:, r, part, i0:i0 + P].rearrange("p (i two) -> p i two", two=2)[:, :, parity]
                            ins = pe.matmul(misc[rows, g * (P // 2):(g + 1) * (P // 2)], pick[:, HA * k + g, part, rows], src,
                                            start=(turn_of == 0), stop=(turn_of == len(parts_of) - 1), skip_group_check=True)
                ins.then_inc(rows_done.sem, 1)

            def use_p(it, c, b, k):
                if k == 0:
                    xn_done.wait(pe, b, 1)
                    for t in range(QPB):
                        ins = pe.transpose(misc[:, t * P:(t + 1) * P], xn[:, t, :], ident[:])
                    ins.then_inc(xT_turned.sem, 1)
                elif k < 3:
                    xT_done.wait(pe, b, 1)
                    pe.matmul(misc[:], (wq, wk)[k - 1][:], xT[:], start=True, stop=True).then_inc(
                        (q_proj, k_proj)[k - 1].sem, 1)
                else:
                    for t in range(QPB):
                        pe.matmul(misc[:, t * P:(t + 1) * P], xT[:, t * P:(t + 1) * P], wv[:], start=True, stop=False)
                        ins = pe.matmul(misc[:, t * P:(t + 1) * P], ones[:], bv[:], start=False, stop=True)
                    ins.then_inc(v_proj.sem, 1)

            def use_e(it, c, k):
                q, b, r = at(it, c), seq(it, c), c // QPB % R2
                i0 = c % QPB * P
                if k == 0:
                    oc_done.wait(pe, q, 1)
                    for s in range(4):
                        ins = pe.transpose(misc[:, s * P:(s + 1) * P], oc[:, s * P:(s + 1) * P], ident[:])
                    ins.then_inc(o_turned.sem, 1)
                elif k == 1:
                    pe.matmul(misc[:, 0:D + H], sigma[:, r, i0:i0 + P], mz[:], start=True, stop=True).then_inc(g_prod.sem, 1)
                elif k == 2:
                    g_step.wait(pe, q, 5)
                    pe.transpose(misc[:, 0:D], mixed[:], ident[:]).then_inc(mixed_turned.sem, 1)
                else:
                    mixedT_done.wait(pe, q, 1)
                    pe.matmul(misc[:, 0:D], mixedT[:], wo[:], start=True, stop=False)
                    pe.matmul(misc[:, 0:D], ones[:], bo[:], start=False, stop=True).then_inc(y_prod.sem, 1)

            def scores(it, c, o):
                q, b, r = at(it, c), seq(it, c), c // QPB % R2
                qdhi_done.wait(pe, q, o * OCT // IB + 1)
                qdlo_done.wait(pe, q, o * OCT // IB + 1)
                if o == 0:
                    klo_done.wait(pe, b, 1)
                    even_done.wait(pe, q, H // HA)
                    odd_done.wait(pe, q, H // HA)
                exp_done.wait(pe, q, o + 1 - RS)
                dst = ps_s[:, o % RS, :]
                hi, lo = (x[:, o * OCT:(o + 1) * OCT, :].rearrange("p i h -> p (i h)") for x in (qd_hi, qd_lo))
                place = c % QPB
                runs = {0: ((HALF, S, False), (0, HALF, True)), QPB - 1: ((0, HALF, False), (HALF, S, True))}.get(
                    place, ((0, S, True),))
                for lo_key, hi_key, near in runs:
                    k_h, k_l = ((x[:, r, lo_key:hi_key] for x in ((k_hi, k_lo) if near else (far_hi, far_lo))))
                    out = dst[:, lo_key:hi_key]
                    pe.matmul(out, hi, k_h, start=True, stop=False, skip_group_check=True)
                    pe.matmul(out, hi, k_l, start=False, stop=False, skip_group_check=True)
                    pe.matmul(out, lo, k_h, start=False, stop=not near, skip_group_check=True)
                near_lo, near_hi = [run[:2] for run in runs if run[2]][0]
                for pair in range(4):
                    i = o * OCT + 2 * pair
                    y = S - (place * P + i)
                    ins = pe.matmul(dst[32 * pair:32 * pair + 32, near_lo:near_hi], qr[:, c % R2, i * H:(i + 2) * H],
                                    window[:, y + near_lo:y + near_hi], start=False, stop=(pair == 3), skip_group_check=True)
                ins.then_inc(s_done.sem, 1)

            def turn(it, c, o):
                q = at(it, c)
                exp_done.wait(pe, q, o + 1)
                if o % 2 == 0:
                    tact_done.wait(pe, q, o // 2)
                else:
                    tdve_done.wait(pe, q, o // 2)
                for kb in range(QPB):
                    ins = pe.transpose(ps_t[:, o % RT, kb * P:(kb + 1) * P], expo[:, o % RS, kb * P:(kb + 1) * P], ident[:])
                ins.then_inc(t_done.sem, 1)

            def values(it, c, j):
                q, b, r = at(it, c), seq(it, c), c // QPB % R2
                s, half = divmod(j, 2)
                if j == 0:
                    tact_done.wait(pe, q, NO // 2)
                    tdve_done.wait(pe, q, NO // 2)
                    v_done.wait(pe, b, 1)
                    oc_done.wait(pe, q, 0)
                for kb in (2 * half, 2 * half + 1):
                    for g in range(4):
                        h = 4 * s + g
                        ins = pe.matmul(ps_v[32 * g:32 * g + 32, s * P:(s + 1) * P],
                                        v[:, r, kb, h * (HD + 1):h * (HD + 1) + 32], probs[:, c % R2, kb, h, :],
                                        start=(kb == 0), stop=(kb == QPB - 1), skip_group_check=True)
                if j == 7:
                    ins.then_inc(pv_done.sem, 1)

            def one(it, c):
                for o in range(NO):
                    for use in uses(it, c, o):
                        misc_free(pe, it, c, use)
                        kind, k = use[:2]
                        if kind == "A":
                            use_a(it, c + 1, k)
                        elif kind == "P":
                            use_p(it, c, projected(it, c), k)
                        else:
                            use_e(it, c - 2, k)
                    if at(it, c) is not None:
                        scores(it, c, o)
                    ct, ot = turned_at(c, o)
                    if at(it, ct) is not None:
                        turn(it, ct, ot)
                    if o in VALUES and at(it, c - 1) is not None:
                        values(it, c - 1, VALUES.index(o))
            run(pe, one)

        def turned_to_probs(eng, copy, it, c, o, done):
            q = at(it, c)
            t_done.wait(eng, q, o + 1)
            if o < 2:
                pv_done.wait(eng, q, -1)
            dst = probs[:, c % R2, :, :, o * OCT:(o + 1) * OCT]
            copy(dst, ps_t[:, o % RT, :].rearrange("p (k i h) -> p k h i", k=QPB, h=H)).then_inc(done.sem, 1)

        @block.scalar
        def _(act):
            def use_a(it, c, k):
                q = at(it, c)
                rows_done.wait(act, q, k + 1)
                if k == 0:
                    s_done.wait(act, q, -NO)
                src = misc[0:ODD, :].rearrange("p (g i) -> p g i", g=HA)
                dst = qr[0:ODD, c % R2, :].rearrange("p (i two h) -> p h i two", two=2, h=H)
                act.copy(dst[:, HA * k:HA * (k + 1), :, 0], src).then_inc(even_done.sem, 1)

            def use_p(it, c, b, k):
                r = (c + 3) // QPB % R2
                if k == 0:
                    xT_turned.wait(act, b, 1)
                    v_proj.wait(act, b, 0)
                    act.copy(xT[:], misc[:]).then_inc(xT_done.sem, 1)
                elif k == 1:
                    q_proj.wait(act, b, 1)
                    qdhi_done.wait(act, at(it, c + 3), -JB * QPB)
                    act.activation(q_hi[:, r, :], misc[:], ACT.Identity, bias=bq[:, 0:1]).then_inc(qhi_done.sem, 1)
                elif k == 2:
                    k_proj.wait(act, b, 1)
                    s_done.wait(act, at(it, c + 3), -NO * QPB)
                    act.activation(k_hi[:, r, :], misc[:], ACT.Identity, bias=bk[:, 0:1])
                    for end, keys in enumerate((slice(0, HALF), slice(HALF, S))):
                        ins = act.activation(far_hi[:, r, keys], misc[:, keys], ACT.Identity, bias=bk_far[:, end:end + 1])
                    ins.then_inc(khi_done.sem, 1)
                else:
                    v_proj.wait(act, b, 1)
                    pv_done.wait(act, at(it, c + 3), -QPB)
                    dst = v[:, r, :, 0:H * (HD + 1)].rearrange("p t (h e) -> p t h e", h=H)[:, :, :, 0:HD]
                    act.copy(dst, misc[:].rearrange("p (t h e) -> p t h e", t=QPB, h=H)).then_inc(v_done.sem, 1)

            def one(it, c):
                for o in range(NO):
                    for kind, k, _ in uses(it, c, o):
                        if kind == "A":
                            use_a(it, c + 1, k)
                        elif kind == "P":
                            use_p(it, c, projected(it, c), k)
                        elif kind == "E" and k == 2:
                            q = at(it, c - 2)
                            mixed_turned.wait(act, q, 1)
                            y_prod.wait(act, q, 0)
                            act.copy(mixedT[:], misc[:, 0:D]).then_inc(mixedT_done.sem, 1)
                    q = at(it, c)
                    if q is not None:
                        max_done.wait(act, q, o + 1)
                        t_done.wait(act, q, o + 1 - RS)
                        act.activation(expo[:, o % RS, :], ps_s[:, o % RS, :], ACT.Exp,
                                       bias=nm[:, o:o + 1]).then_inc(exp_done.sem, 1)
                    ct, ot = turned_at(c, o)
                    if ot % 2 == 0 and at(it, ct) is not None:
                        turned_to_probs(act, act.copy, it, ct, ot, tact_done)
                    if o == 13 and projected(it, c) is not None:
                        b = projected(it, c)
                        split.wait(act, b, 5)
                        act.activation(eneg[:], neg[:], ACT.Exp).then_inc(neg_exp.sem, 1)
            run(act, one)

        @block.gpsimd
        def _(pool):
            heads = head_of[:].rearrange("p (a h) -> p a h", a=1).broadcast_to([P, IB, H])

            def expand(it, c, jb, src, dst, done):
                i0 = c % QPB * P + jb * IB
                x = src[:, c // QPB % R2, i0:i0 + IB].bitcast(F32).rearrange("p (i a) -> p i a", a=1).broadcast_to([P, IB, H])
                pool.tensor_tensor(dst[:, jb * IB:(jb + 1) * IB, :], x, heads, ALU.mult).then_inc(done.sem, 1)

            def one(it, c):
                b = projected(it, c)
                q = at(it, c + 1)
                for jb in range(JB):
                    if q is not None:
                        qlo_done.wait(pool, seq(it, c + 1), 1)
                        s_done.wait(pool, q, -NO + (jb + 1) * NO // JB)
                        expand(it, c + 1, jb, q_hi, qd_hi, qdhi_done)
                        expand(it, c + 1, jb, q_lo, qd_lo, qdlo_done)
                if b is not None:
                    r = (c + 3) // QPB % R2
                    q32_done.wait(pool, b, 1)
                    qhi_done.wait(pool, b, 1)
                    pool.tensor_tensor(q_lo[:, r, :], q32[:], q_hi[:, r, :].bitcast(F32), ALU.subtract).then_inc(qlo_done.sem, 1)
            run(pool, one)

        @block.vector
        def _(dve):
            def use_a(it, c, k):
                q = at(it, c)
                rows_done.wait(dve, q, k + 1)
                if k == 0:
                    s_done.wait(dve, q, -NO)
                src = misc[ODD:P, :].rearrange("p (g i) -> p g i", g=HA)
                dst = qr[ODD:P, c % R2, :].rearrange("p (i two h) -> p h i two", two=2, h=H)
                dve.tensor_copy(dst[:, HA * k:HA * (k + 1), :, 1], src).then_inc(odd_done.sem, 1)

            def use_p(it, c, b, k):
                r = (c + 3) // QPB % R2
                if k == 1:
                    q_proj.wait(dve, b, 1)
                    qlo_done.wait(dve, b, 0)
                    qhi_done.wait(dve, b, 1)
                    dve.tensor_scalar(q32[:], misc[:], bq[:, 0:1], None, ALU.add).then_inc(q32_done.sem, 1)
                elif k == 2:
                    khi_done.wait(dve, b, 1)
                    dve.scalar_tensor_tensor(out=k_lo[:, r, :], in0=misc[:], scalar=bk[:, 0:1],
                                             in1=k_hi[:, r, :].bitcast(F32), op0=ALU.add, op1=ALU.subtract)
                    for end, keys in enumerate((slice(0, HALF), slice(HALF, S))):
                        ins = dve.scalar_tensor_tensor(out=far_lo[:, r, keys], in0=misc[:, keys], scalar=bk_far[:, end:end + 1],
                                                       in1=far_hi[:, r, keys].bitcast(F32), op0=ALU.add, op1=ALU.subtract)
                    ins.then_inc(klo_done.sem, 1)

            def query_parts(it, c, b):
                r = (c + 3) // QPB % R2
                q32_done.wait(dve, b, 1)
                rows_done.wait(dve, at(it, c + 3), -(H // HA) * QPB)
                dve.tensor_copy(q_part[:, r, 0, :], q32[:]).then_inc(split.sem, 1)
                split.wait(dve, b, 1)
                dve.tensor_tensor(rest[:], q32[:], q_part[:, r, 0, :], ALU.subtract).then_inc(split.sem, 1)
                split.wait(dve, b, 2)
                dve.tensor_copy(q_part[:, r, 1, :], rest[:]).then_inc(split.sem, 1)
                split.wait(dve, b, 3)
                dve.tensor_tensor(q_part[:, r, 2, :], rest[:], q_part[:, r, 1, :], ALU.subtract).then_inc(split.sem, 1)
                dve.tensor_scalar(neg[:], q32[:], 0.0, None, ALU.min).then_inc(split.sem, 1)

            def finish_sigma(it, c, b):
                r = (c + 3) // QPB % R2
                neg_exp.wait(dve, b, 1)
                g_prod.wait(dve, at(it, c + 3), -QPB)
                dve.scalar_tensor_tensor(out=sigma[:, r, :], in0=q32[:], scalar=0.0, in1=eneg[:], op0=ALU.max,
                                         op1=ALU.add).then_inc(split.sem, 1)

            def use_e(it, c, k):
                q = at(it, c)
                turned = misc[:].rearrange("p (h e) -> p h e", e=32)
                by_head = lambda x: x[:].rearrange("p (h e) -> p h e", h=H)
                spreadh = lambda x: x[:].broadcast_to([P, H, HD])
                if k == 0:
                    o_turned.wait(dve, q, 1)
                    g_step.wait(dve, q, 0)
                    dve.reciprocal(rden[:], turned[:, :, HD:HD + 1]).then_inc(o_step.sem, 1)
                    o_step.wait(dve, q, 1)
                    dve.tensor_scalar(rdeng[:], rden[:], gate[:, 2:3], None, ALU.mult).then_inc(o_step.sem, 1)
                    o_step.wait(dve, q, 2)
                    dve.tensor_tensor(by_head(local), turned[:, :, 0:HD], spreadh(rdeng), ALU.mult).then_inc(o_step.sem, 1)
                elif k == 1:
                    g_prod.wait(dve, q, 1)
                    dve.tensor_scalar(gden[:], misc[:, D:D + H], 1e-6, None, ALU.add).then_inc(g_step.sem, 1)
                    g_step.wait(dve, q, 1)
                    dve.reciprocal(grden[:], gden[:]).then_inc(g_step.sem, 1)
                    g_step.wait(dve, q, 2)
                    dve.tensor_scalar(grdeng[:], grden[:], gate[:, 3:4], None, ALU.mult).then_inc(g_step.sem, 1)
                    g_step.wait(dve, q, 3)
                    dve.tensor_tensor(by_head(glob), misc[:, 0:D].rearrange("p (h e) -> p h e", h=H), spreadh(grdeng),
                                      ALU.mult).then_inc(g_step.sem, 1)
                    g_step.wait(dve, q, 4)
                    mixed_turned.wait(dve, q, 0)
                    dve.tensor_tensor(mixed[:], local[:], glob[:], ALU.add).then_inc(g_step.sem, 1)
                elif k == 3:
                    row = X[:, bass.ds(q, 1), :].rearrange("p a d -> p (a d)")
                    y_prod.wait(dve, q, 1)
                    dve.tensor_tensor(y[:], misc[:, 0:D], row, ALU.add).then_inc(y_done.sem, 1)
                    y_done.wait(dve, q, 1)
                    dve.tensor_scalar(row, y[:], 0.0, None, ALU.add)
                    dve.bn_stats(STATS[:, bass.ds(q, 1), :].rearrange("p a d -> p (a d)"), y[:])

            def maximum(it, c, o):
                q = at(it, c)
                s_done.wait(dve, q, o + 1)
                dve.tensor_reduce(nm[:, o:o + 1], ps_s[:, o % RS, :], AX.X, ALU.max, negate=True).then_inc(max_done.sem, 1)

            def one(it, c):
                b = projected(it, c)
                if b is not None:
                    xT_turned.wait(dve, b, 0)
                    for t in range(QPB):
                        row = at(it, c + 3 + t)
                        ins = dve.tensor_scalar(xn[:, t, :], X[:, bass.ds(row, 1), :].rearrange("p a d -> p (a d)"),
                                                mean[:, bass.ds(row, 1), :].rearrange("p a d -> p (a d)"),
                                                rstd[:, bass.ds(row, 1), :].rearrange("p a d -> p (a d)"),
                                                ALU.subtract, ALU.mult)
                    ins.then_inc(xn_done.sem, 1)
                q = at(it, c - 2)
                if q is not None:
                    pv_done.wait(dve, q, 1)
                    o_turned.wait(dve, q, 0)
                    dve.tensor_copy(oc[:], ps_v[:]).then_inc(oc_done.sem, 1)
                for o in range(NO):
                    for kind, k, _ in uses(it, c, o):
                        if kind == "A":
                            use_a(it, c + 1, k)
                        elif kind == "P":
                            use_p(it, c, b, k)
                        else:
                            use_e(it, c - 2, k)
                    if at(it, c) is not None:
                        maximum(it, c, o)
                    ct, ot = turned_at(c, o)
                    if ot % 2 == 1 and at(it, ct) is not None:
                        turned_to_probs(dve, dve.tensor_copy, it, ct, ot, tdve_done)
                    if b is not None and o == 11:
                        query_parts(it, c, b)
                    if b is not None and o == 15:
                        finish_sigma(it, c, b)
            run(dve, one)


def load_phase(nc, io, X, STATS):
    D = X.shape[2]
    ROWS = X.shape[1]
    PIECE = 4
    with ExitStack() as ctx:
        NQ = ROWS // PIECE
        x_in = [ctx.enter_context(nc.semaphore(f"x_in{k}")) for k in range(NQ)]
        block = ctx.enter_context(nc.Block())

        @block.sync
        def _(sp):
            for i in range(ROWS // PIECE):
                sp.dma_start(X[:, i * PIECE:(i + 1) * PIECE, :], io["x"][:, i * PIECE:(i + 1) * PIECE, :]).then_inc(x_in[i % NQ], 16)

        @block.vector
        def _(dve):
            for i in range(ROWS // PIECE):
                dve.wait_ge(x_in[i % NQ], 16 * (i // NQ + 1))
                for t in range(PIECE):
                    dve.bn_stats(STATS[:, i * PIECE + t, :], X[:, i * PIECE + t, :])


def macaron_layer(nc, io, out):
    D = io["x"].shape[2]
    ROWS = io["x"].shape[1]
    with ExitStack() as ctx:
        X = ctx.enter_context(nc.sbuf_tensor("X", [P, ROWS, D], F32))
        STATS = ctx.enter_context(nc.sbuf_tensor("STATS", [P, ROWS, 6], F32))
        load_phase(nc, io, X, STATS)
        ffn_phase(nc, io, X, STATS, "ffn1", None)
        attention_phase(nc, io, X, STATS)
        ffn_phase(nc, io, X, STATS, "ffn2", out)


def _shape_constants():
    import numpy as _np

    heads, hd = 16, 8
    bands = (((1, 1), (1, 2), (1, 3)), ((2, 1), (2, 2), (3, 1))) * 2
    head_of = _np.kron(_np.eye(heads), _np.ones((hd, 1))).astype(_np.float32)
    spread = _np.zeros((128, 3, 128), _np.float32)
    emb_part = _np.zeros((128, 3), _np.float32)
    for band in range(4):
        for n, (q_part, e_part) in enumerate(bands[band]):
            for d in range(hd):
                row = 32 * band + hd * n + d
                spread[d::hd, q_part - 1, row] = 1.0
                emb_part[row, e_part - 1] = 1.0
    return {"head_of": head_of, "spread": spread, "emb_part": emb_part}


def kernel(**inputs):
    import numpy as _np
    import concourse.bacc as _bacc
    from concourse import mybir as _mybir
    from concourse.bass_utils import run_bass_kernel_spmd as _run

    nc = _bacc.Bacc("TRN2", target_bir_lowering=False, num_devices=1)
    x = _np.asarray(inputs["L0_attn_hidden_states"])
    f, a = "L0_ffn_", "L0_attn_"
    host = {
        "x": x.reshape(-1, 128, x.shape[-1]),
        "router": inputs[f + "router_DE"],
        "w_in": inputs[f + "w_in_eDF"],
        "w_gate": inputs[f + "w_swiglu_eDF"],
        "w_out": inputs[f + "w_out_eFD"],
        "w_in_s": _np.asarray(inputs[f + "w_in_shared_FD"]).T,
        "w_gate_s": _np.asarray(inputs[f + "w_swiglu_FD"]).T,
        "w_out_s": _np.asarray(inputs[f + "w_out_shared_DF"]).T,
        "ident": _np.eye(128, dtype=_np.float32),
        "wq": _np.asarray(inputs[a + "Wq"]).T,
        "wk": _np.asarray(inputs[a + "Wk"]).T,
        "wv": _np.asarray(inputs[a + "Wv"]).T,
        "wo": _np.asarray(inputs[a + "Wo"]).T,
        "bq": _np.asarray(inputs[a + "bq"]).reshape(128, 1),
        "bk": _np.asarray(inputs[a + "bk"]).reshape(128, 1),
        "bv": _np.asarray(inputs[a + "bv"]).reshape(1, 128),
        "bo": _np.asarray(inputs[a + "bo"]).reshape(1, 128),
        "M": inputs[a + "M"],
        "z": _np.asarray(inputs[a + "z"]).reshape(128, 1),
        "alpha": _np.asarray(inputs[a + "gate_alpha"]).reshape(1, 1),
        "rel": _np.tile(_np.asarray(inputs[a + "rel_emb"])[::-1].T, (16, 1)),
        **_shape_constants(),
        "ranks": _np.tile(_np.arange(8, 0, -1, dtype=_np.float32), (128, 4, 1)),
    }
    arrays, io = {}, {}
    for name, a in host.items():
        a = _np.ascontiguousarray(a)
        arrays["in_" + name] = a
        io[name] = nc.dram_tensor("in_" + name, a.shape, _mybir.dt.from_np(a.dtype), kind="ExternalInput").ap()
    io["alpha"] = io["alpha"].broadcast_to([128, 1])
    io["x"] = io["x"].rearrange("r p d -> p r d")
    out = nc.dram_tensor("out_0", x.shape, _mybir.dt.float32, kind="ExternalOutput").ap()
    macaron_layer(nc, io, out.rearrange("b (r p) d -> p (b r) d", p=128))
    r = _run(nc, [arrays], core_ids=[0])
    return r.results[0]["out_0"]
```

```python
from contextlib import ExitStack

import concourse.bass as bass
from concourse import mybir

P = 128
F32, F32R, BF16, U32 = mybir.dt.float32, mybir.dt.float32r, mybir.dt.bfloat16, mybir.dt.uint32
ALU, ACT, AX = mybir.AluOpType, mybir.ActivationFunctionType, mybir.AxisListType
EPS = 1e-5


class Ring:

    def __init__(self, sem, per):
        self.sem, self.per = sem, per

    def at(self, n, c):
        return n * self.per + c

    def wait(self, eng, n, c):
        if isinstance(n, int) and n * self.per + c <= 0:
            return
        eng.wait_ge(self.sem, n * self.per + c)


def mean_and_variance(dve, STATS, work, done):
    D = P
    dve.tensor_tensor(work[0], STATS[:, :, 1:2], STATS[:, :, 4:5], ALU.add).then_inc(done.sem, 1)
    dve.tensor_tensor(work[1], STATS[:, :, 1:2], STATS[:, :, 4:5], ALU.subtract).then_inc(done.sem, 1)
    dve.tensor_tensor(work[5], STATS[:, :, 2:3], STATS[:, :, 5:6], ALU.add).then_inc(done.sem, 1)
    dve.wait_ge(done.sem, 1)
    dve.tensor_scalar(work[2], work[0], 0.5, None, ALU.mult).then_inc(done.sem, 1)
    dve.wait_ge(done.sem, 2)
    dve.tensor_scalar(work[3], work[1], 0.5, None, ALU.mult).then_inc(done.sem, 1)
    dve.wait_ge(done.sem, 5)
    dve.tensor_tensor(work[4], work[3], work[3], ALU.mult).then_inc(done.sem, 1)
    dve.wait_ge(done.sem, 6)
    dve.scalar_tensor_tensor(out=work[6], in0=work[5], scalar=1.0 / D, in1=work[4], op0=ALU.mult, op1=ALU.add).then_inc(done.sem, 1)
    dve.wait_ge(done.sem, 7)


def ffn_phase(nc, io, X, STATS, tag, store, meanwhile=None):
    D, E, F = P, io["router"].shape[1], io["w_in"].shape[2]
    NE, C = E + 1, F // P
    U = NE * C
    T = 4
    N = X.shape[1] // T
    W = T * P
    R = 2
    RH = 6
    RE = 4
    RAW = 8
    DELAY = 4
    NEXT = U - 8
    SCALED = {0: 2, 1: 3, 2: 4, 3: 5, 4: 6, 5: 7, 6: 8}
    GATED = {NEXT + 4: (0,), NEXT + 5: (1,), NEXT + 6: (2, 3)}
    LOW = 3
    assert E % R == 0 and U % RH == 0 and U % 2 == 0 and E % RE == 0

    with ExitStack() as ctx:
        def sb(name, shape, dt):
            return ctx.enter_context(nc.sbuf_tensor(f"{tag}_{name}", shape, dt))

        def ps(name, shape, dt=F32):
            return ctx.enter_context(nc.psum_tensor(f"{tag}_{name}", shape, dt))

        def ring(name, per):
            return Ring(ctx.enter_context(nc.semaphore(f"{tag}_{name}")), per)

        raw = sb("raw", [P, RAW, max(C * D, F)], F32)
        w_mid = sb("w_mid", [P, 2, NE, F], F32R)
        w_gate = sb("w_gate", [P, 2, NE, F], F32R)
        w_out = sb("w_out", [P, 2, NE, C, D], F32R)
        router32 = sb("router32", [P, E], F32)
        router = sb("router", [P, 2, E], F32R)
        partial = sb("partial", [P, W], F32)
        ident = sb("ident", [P, P], F32)
        ranks_sb = sb("ranks_sb", [P, T, E], F32)
        ranks = ranks_sb[:]
        rstd = sb("rstd", [P, N * T, 1], F32)
        std = sb("std", [P, N * T, 1], F32)
        eps, warm = sb("eps", [P, 1], F32), sb("warm", [P, 1], F32)
        moments = sb("moments", [P, 7, N * T, 1], F32)
        mean, var = moments[:, 2], moments[:, 6]
        xn = sb("xn", [P, T, D], F32)
        xe = sb("xe", [P, RE, T, D], F32)
        xT_hi = sb("xT_hi", [P, R + 1, W], F32R)
        xT_lo = sb("xT_lo", [P, R + 1, W], F32R)
        silu = sb("silu", [P, RH, W], F32)
        h = sb("h", [P, RH, W], F32)
        h_hi = sb("h_hi", [P, RH, W], F32R)
        h_lo = sb("h_lo", [P, RH, W], F32R)
        scores = sb("scores", [P, T, E], F32)
        tanh = sb("tanh", [P, T, E], F32)
        top = sb("top", [P, 2, T, 1], F32)
        lead = sb("lead", [P, T, 1], F32)
        rest = sb("rest", [P, T, E], F32)
        order = sb("order", [P, T, E], F32)
        pick = sb("pick", [P, 2, T, E], F32)
        gate = sb("gate", [P, T, E], F32)
        oT = sb("oT", [P, W], F32)
        y = sb("y", [P, T, D], F32)

        ps_x = ps("ps_x", [P, 2, W])
        ps_mid = ps("ps_mid", [P, 2, W])
        ps_gate = ps("ps_gate", [P, 2, W])
        ps_out = ps("ps_out", [P, W])
        ps_misc = ps("ps_misc", [P, W])

        const_in = ring("const_in", 0)
        raw_in = [ring(f"raw_in{k}", 0) for k in range(RAW)]
        w_hi = ring("w_hi", 0)
        split = ring("split", 0)
        consts = ring("consts", 0)
        stats_done = ring("stats_done", 0)
        sqrt_done = ring("sqrt_done", 0)
        rstd_done = ring("rstd_done", 0)
        xn_done = ring("xn_done", 1)
        x0_turned = ring("x0_turned", 1)
        x0hi_done = ring("x0hi_done", 1)
        x0lo_done = ring("x0lo_done", 1)
        xT_done = ring("xT_done", E)
        xhi_done = ring("xhi_done", E)
        xlo_done = ring("xlo_done", E)
        part_scored = ring("part_scored", 1)
        part_out = ring("part_out", 1)
        routed = ring("routed", 1)
        tanh_done = ring("tanh_done", 1)
        chain = ring("chain", 16)
        xe_done = ring("xe_done", E)
        mid_done = ring("mid_done", U)
        silu_done = ring("silu_done", U)
        h_done = ring("h_done", U)
        hhi_done = ring("hhi_done", U)
        hlo_pool = ring("hlo_pool", U - U // LOW)
        hlo_dve = ring("hlo_dve", U // LOW)
        out_done = ring("out_done", U)
        oT_done = ring("oT_done", 1)
        turned = ring("turned", 1)
        y_done = ring("y_done", 2)
        stored = ring("stored", 16)

        def low_wait(eng, n, u):
            v, n = (u, n) if u >= 0 else (u + U, n - 1)
            if v % LOW == LOW - 1:
                hlo_dve.wait(eng, n, v // LOW + 1)
            else:
                hlo_pool.wait(eng, n, v - v // LOW + 1)

        block = ctx.enter_context(nc.Block())

        weights = [(io["w_in_s"], w_mid[:, :, 0, :]), (io["w_gate_s"], w_gate[:, :, 0, :]),
                   (io["w_out_s"].rearrange("(c p) d -> p c d", p=P), w_out[:, :, 0])]
        for e in range(E):
            weights += [(io["w_in"][e], w_mid[:, :, e + 1, :]), (io["w_gate"][e], w_gate[:, :, e + 1, :]),
                        (io["w_out"][e].rearrange("(c p) d -> p c d", p=P), w_out[:, :, e + 1])]

        def weights_in(u):
            return [i for i in range(3 + 3 * u // 2 + u % 2, 3 + 3 * (u + 1) // 2 + (u + 1) % 2) if i < len(weights)]

        def shaped(ap, to):
            return ap.rearrange("p (c d) -> p c d", c=C) if len(to.shape) == 4 else ap

        @block.sync
        def _(sp):
            for i, (src, to) in enumerate(weights):
                if i == 3:
                    for to_const, const in ((ident[:], "ident"), (router32[:], "router"), (ranks, "ranks")):
                        sp.dma_start(to_const, io[const]).then_inc(const_in.sem, 16)
                if i >= RAW:
                    sp.wait_ge(split.sem, i - RAW + 1)
                sp.dma_start(shaped(raw[:, i % RAW, :], to), src).then_inc(raw_in[i % RAW].sem, 16)
            if store is not None:
                with sp.Fori(0, N) as n:
                    sp.wait_ge(y_done.sem, y_done.at(n, 2))
                    sp.dma_start(store[:, bass.ts(n, T), :], X[:, bass.ts(n, T), :]).then_inc(stored.sem, 16)
                sp.wait_ge(stored.sem, 16 * N)

        @block.tensor
        def _(pe):
            def product(out, lhs, rhs, start, stop):
                for i, (a, b) in enumerate(((0, 0), (0, 1), (1, 0))):
                    ins = pe.matmul(out, lhs(a), rhs(b), start=start and i == 0, stop=stop and i == 2)
                return ins

            def turn_unscaled(n):
                pe.wait_ge(xn_done.sem, xn_done.at(n, 1))
                y_done.wait(pe, n, -3)
                for t in range(T):
                    ins = pe.transpose(ps_misc[:, t * P:(t + 1) * P], xn[:, t, :], ident[:])
                ins.then_inc(x0_turned.sem, 1)

            def turn_in(n, e):
                pe.wait_ge(xe_done.sem, xe_done.at(n, e))
                xlo_done.wait(pe, n, e - 2)
                for t in range(T):
                    ins = pe.transpose(ps_x[:, e % 2, t * P:(t + 1) * P], xe[:, e % RE, t, :], ident[:])
                ins.then_inc(xT_done.sem, 1)

            def route(n):
                pe.wait_ge(x0lo_done.sem, x0lo_done.at(n, 1))
                parts = router[:].rearrange("p a e -> p (a e)")
                for i, x in enumerate((xT_hi, xT_lo)):
                    ins = pe.matmul(ps_misc[0:2 * E, :], parts, x[:, R, :], start=(i == 0), stop=(i == 1))
                ins.then_inc(part_scored.sem, 1)

            def turn_scores(n):
                pe.wait_ge(part_out.sem, part_out.at(n, 1))
                for t in range(T):
                    ins = pe.transpose(ps_misc[:, t * P:(t + 1) * P], partial[:, t * P:(t + 1) * P], ident[:])
                ins.then_inc(routed.sem, 1)

            def unit(n, u):
                e, c = divmod(u, C)
                if e == 0:
                    pe.wait_ge(x0lo_done.sem, x0lo_done.at(n, 1))
                else:
                    pe.wait_ge(xlo_done.sem, xlo_done.at(n, e))
                h_done.wait(pe, n, u - 1)
                for w, dst in ((w_mid, ps_mid), (w_gate, ps_gate)):
                    ins = product(dst[:, u % 2, :], lambda a: w[:, a, e, c * P:(c + 1) * P],
                                  lambda b: (xT_hi, xT_lo)[b][:, e % R if e else R, :], True, True)
                ins.then_inc(mid_done.sem, 1)

            def output(n, u):
                e, c = divmod(u, C)
                pe.wait_ge(hhi_done.sem, hhi_done.at(n, u + 1))
                low_wait(pe, n, u)
                if u == 0:
                    oT_done.wait(pe, n, 0)
                product(ps_out[:], lambda a: w_out[:, a, e, c, :], lambda b: (h_hi, h_lo)[b][:, u % RH, :],
                        u == 0, u == U - 1).then_inc(out_done.sem, 1)

            def turn_out(n):
                pe.wait_ge(oT_done.sem, oT_done.at(n, 1))
                if n_has_next(n):
                    pe.wait_ge(chain.sem, chain.at(n + 1, 2))
                for t in range(T):
                    ins = pe.transpose(ps_misc[:, t * P:(t + 1) * P], oT[:, t * P:(t + 1) * P], ident[:])
                ins.then_inc(turned.sem, 1)

            def tile(n, first, last):
                for u in range(U):
                    e, c = divmod(u, C)
                    if u == DELAY + 1 and not first:
                        turn_out(n - 1)
                    if c == 0 and 0 < e < NE - 1 or u == 1:
                        turn_in(n, e + 1)
                    if u == NEXT and not last:
                        turn_unscaled(n + 1)
                    if u == NEXT + 2 and not last:
                        route(n + 1)
                    if u == NEXT + 4 and not last:
                        turn_scores(n + 1)
                    if first:
                        pe.wait_ge(split.sem, 3 * (e + 1))
                    unit(n, u)
                    if u >= DELAY:
                        output(n, u - DELAY)
                    elif not first:
                        output(n - 1, u - DELAY + U)

            def n_has_next(n):
                return not (isinstance(n, int) and n == N - 1)

            pe.wait_ge(const_in.sem, 48)
            turn_unscaled(0)
            pe.wait_ge(consts.sem, 3)
            route(0)
            turn_scores(0)
            tile(0, True, False)
            with pe.Fori(1, N - 1) as n:
                tile(n, False, False)
            tile(N - 1, False, True)
            for u in range(U - DELAY, U):
                output(N - 1, u)
            turn_out(N - 1)

        @block.scalar
        def _(act):
            def unscaled_high(n):
                act.wait_ge(x0_turned.sem, x0_turned.at(n, 1))
                mid_done.wait(act, n - 1, C)
                act.copy(xT_hi[:, R, :], ps_misc[:]).then_inc(x0hi_done.sem, 1)

            def x_high(n, e):
                act.wait_ge(xT_done.sem, xT_done.at(n, e))
                mid_done.wait(act, n, C * (e - 1))
                act.copy(xT_hi[:, e % R, :], ps_x[:, e % 2, :]).then_inc(xhi_done.sem, 1)

            def h_high(n, u):
                act.wait_ge(h_done.sem, h_done.at(n, u + 1))
                out_done.wait(act, n, u - RH + 1)
                act.copy(h_hi[:, u % RH, :], h[:, u % RH, :]).then_inc(hhi_done.sem, 1)

            def leave(n):
                act.wait_ge(out_done.sem, out_done.at(n, U))
                turned.wait(act, n, 0)
                act.copy(oT[:], ps_out[:]).then_inc(oT_done.sem, 1)

            def partial_out(n):
                act.wait_ge(part_scored.sem, part_scored.at(n, 1))
                routed.wait(act, n, 0)
                act.copy(partial[0:2 * E, :], ps_misc[0:2 * E, :]).then_inc(part_out.sem, 1)

            def gates(n):
                act.wait_ge(chain.sem, chain.at(n, 2))
                act.activation(tanh[:], scores[:], ACT.Tanh, scale=0.5).then_inc(tanh_done.sem, 1)

            def weight_high(i):
                to = weights[i][1]
                act.wait_ge(raw_in[i % RAW].sem, 16 * (i // RAW + 1))
                act.copy(to[:, 0], shaped(raw[:, i % RAW, :], to)).then_inc(w_hi.sem, 1)

            def tile(n, first, last):
                for u in range(U):
                    e, c = divmod(u, C)
                    if first:
                        for i in weights_in(u):
                            weight_high(i)
                    if u == DELAY and not first:
                        leave(n - 1)
                    if c == 0 and 0 < e < NE - 1 or u == 1:
                        x_high(n, e + 1)
                    if u == NEXT and not last:
                        unscaled_high(n + 1)
                    if u == NEXT + 3 and not last:
                        partial_out(n + 1)
                    if u == NEXT + 6 and not last:
                        gates(n + 1)
                    if u > 0:
                        h_high(n, u - 1)
                    elif not first:
                        h_high(n - 1, U - 1)
                    act.wait_ge(mid_done.sem, mid_done.at(n, u + 1))
                    h_done.wait(act, n, u - RH + 1)
                    act.activation(silu[:, u % RH, :], ps_mid[:, u % 2, :], ACT.Silu).then_inc(silu_done.sem, 1)

            act.wait_ge(consts.sem, 1)
            act.activation(warm[:], eps[:], ACT.Sqrt)
            act.wait_ge(stats_done.sem, 7)
            act.activation(std[:], var, ACT.Sqrt, bias=eps[:, 0:1]).then_inc(sqrt_done.sem, 1)
            for i in range(3):
                weight_high(i)
            unscaled_high(0)
            partial_out(0)
            gates(0)
            tile(0, True, False)
            with act.Fori(1, N - 1) as n:
                tile(n, False, False)
            tile(N - 1, False, True)
            h_high(N - 1, U - 1)
            leave(N - 1)

        @block.gpsimd
        def _(pool):
            def scale(n, e):
                pool.wait_ge(chain.sem, chain.at(n, 16))
                xT_done.wait(pool, n, e - RE + 1)
                pool.tensor_tensor(xe[:, e % RE], xn[:], gate[:, :, e - 1:e].broadcast_to([P, T, D]),
                                   ALU.mult).then_inc(xe_done.sem, 1)

            def h_low(n, u):
                pool.wait_ge(hhi_done.sem, hhi_done.at(n, u + 1))
                out_done.wait(pool, n, u - RH + 1)
                pool.tensor_tensor(h_lo[:, u % RH, :], h[:, u % RH, :], h_hi[:, u % RH, :].bitcast(F32),
                                   ALU.subtract).then_inc(hlo_pool.sem, 1)

            def tile(n, first, last):
                for u in range(U):
                    if u == U - 1 and not last:
                        scale(n + 1, 1)
                    if u % LOW:
                        h_low(n, u - 1)
                    if u in SCALED:
                        scale(n, SCALED[u])

            scale(0, 1)
            tile(0, True, False)
            with pool.Fori(1, N - 1) as n:
                tile(n, False, False)
            tile(N - 1, False, True)

        @block.vector
        def _(dve):
            def normalise(n):
                xe_done.wait(dve, n, 0)
                for t in range(T):
                    r = n * T + t
                    ins = dve.tensor_scalar(xn[:, t, :], X[:, bass.ds(r, 1), :].rearrange("p a d -> p (a d)"),
                                            mean[:, bass.ds(r, 1), :].rearrange("p a d -> p (a d)"),
                                            rstd[:, bass.ds(r, 1), :].rearrange("p a d -> p (a d)"),
                                            ALU.subtract, ALU.mult)
                ins.then_inc(xn_done.sem, 1)

            def unscaled_low(n):
                dve.wait_ge(x0hi_done.sem, x0hi_done.at(n, 1))
                dve.tensor_tensor(xT_lo[:, R, :], ps_misc[:], xT_hi[:, R, :].bitcast(F32),
                                  ALU.subtract).then_inc(x0lo_done.sem, 1)

            def x_low(n, e):
                dve.wait_ge(xhi_done.sem, xhi_done.at(n, e))
                dve.tensor_tensor(xT_lo[:, e % R, :], ps_x[:, e % 2, :], xT_hi[:, e % R, :].bitcast(F32),
                                  ALU.subtract).then_inc(xlo_done.sem, 1)

            def gates(n, part):
                k, half = divmod(part, 2)
                left = (scores, rest)[k]
                c = 2 + 6 * k
                if part == 0:
                    dve.wait_ge(routed.sem, routed.at(n, 1))
                    xe_done.wait(dve, n, 0)
                    by_part = ps_misc[:].rearrange("p (t a e) -> p t a e", t=T, e=E)
                    dve.tensor_copy(scores[:], by_part[:, :, 0]).then_inc(chain.sem, 1)
                    dve.wait_ge(chain.sem, chain.at(n, 1))
                    dve.tensor_tensor(scores[:], scores[:], by_part[:, :, 1], ALU.add).then_inc(chain.sem, 1)
                if half == 0:
                    dve.wait_ge(chain.sem, chain.at(n, c))
                    dve.tensor_reduce(top[:, k], left[:], AX.X, ALU.max).then_inc(chain.sem, 1)
                    dve.wait_ge(chain.sem, chain.at(n, c + 1))
                    dve.tensor_tensor(pick[:, k], left[:], top[:, k].broadcast_to([P, T, E]), ALU.is_equal).then_inc(chain.sem, 1)
                    dve.wait_ge(chain.sem, chain.at(n, c + 2))
                    dve.tensor_tensor(order[:], pick[:, k], ranks, ALU.mult).then_inc(chain.sem, 1)
                    return
                dve.wait_ge(chain.sem, chain.at(n, c + 3))
                dve.tensor_reduce(lead[:], order[:], AX.X, ALU.max).then_inc(chain.sem, 1)
                dve.wait_ge(chain.sem, chain.at(n, c + 4))
                dve.tensor_tensor(pick[:, k], ranks, lead[:].broadcast_to([P, T, E]), ALU.is_equal).then_inc(chain.sem, 1)
                dve.wait_ge(chain.sem, chain.at(n, c + 5))
                if k == 0:
                    dve.scalar_tensor_tensor(out=rest[:], in0=pick[:, 0], scalar=-3e38, in1=scores[:],
                                             op0=ALU.mult, op1=ALU.add).then_inc(chain.sem, 1)
                else:
                    dve.tensor_tensor(order[:], pick[:, 0], pick[:, 1], ALU.add).then_inc(chain.sem, 1)
                    dve.wait_ge(tanh_done.sem, tanh_done.at(n, 1))
                    dve.tensor_scalar(tanh[:], tanh[:], 0.5, 0.5, ALU.mult, ALU.add).then_inc(chain.sem, 1)
                    dve.wait_ge(chain.sem, chain.at(n, 15))
                    dve.tensor_tensor(gate[:], tanh[:], order[:], ALU.mult).then_inc(chain.sem, 1)

            def h_low(n, u):
                dve.wait_ge(hhi_done.sem, hhi_done.at(n, u + 1))
                out_done.wait(dve, n, u - RH + 1)
                dve.tensor_tensor(h_lo[:, u % RH, :], h[:, u % RH, :], h_hi[:, u % RH, :].bitcast(F32),
                                  ALU.subtract).then_inc(hlo_dve.sem, 1)

            def residual(n):
                dve.wait_ge(turned.sem, turned.at(n, 1))
                rows = X[:, bass.ds(n * T, T), :].rearrange("p t d -> p (t d)")
                flat = y[:].rearrange("p t d -> p (t d)")
                dve.scalar_tensor_tensor(out=flat, in0=ps_misc[:], scalar=0.5, in1=rows, op0=ALU.mult,
                                         op1=ALU.add).then_inc(y_done.sem, 1)
                dve.wait_ge(y_done.sem, y_done.at(n, 1))
                dve.tensor_scalar(rows, flat, 0.0, None, ALU.add).then_inc(y_done.sem, 1)
                for t in range(T):
                    dve.bn_stats(STATS[:, bass.ds(n * T + t, 1), :].rearrange("p a d -> p (a d)"), y[:, t, :])

            def weight_low(i):
                to = weights[i][1]
                dve.wait_ge(w_hi.sem, i + 1)
                dve.tensor_tensor(to[:, 1], shaped(raw[:, i % RAW, :], to), to[:, 0].bitcast(F32),
                                  ALU.subtract).then_inc(split.sem, 1)

            def tile(n, first, last):
                for u in range(U):
                    e, c = divmod(u, C)
                    if first:
                        for i in weights_in(u):
                            weight_low(i)
                    if c == 0 and 0 < e < NE - 1 or u == 1:
                        x_low(n, e + 1)
                    if u == NEXT and not last:
                        unscaled_low(n + 1)
                    dve.wait_ge(silu_done.sem, silu_done.at(n, u + 1))
                    hhi_done.wait(dve, n, u - RH + 1)
                    low_wait(dve, n, u - RH)
                    dve.tensor_tensor(h[:, u % RH, :], silu[:, u % RH, :], ps_gate[:, u % 2, :],
                                      ALU.mult).then_inc(h_done.sem, 1)
                    if u % LOW == 0 and (u > 0 or not first):
                        h_low(*((n, u - 1) if u > 0 else (n - 1, U - 1)))
                    if u == DELAY + 2 and not first:
                        residual(n - 1)
                    if last and meanwhile is not None:
                        meanwhile(dve, u)
                    if u == NEXT - 3 and not last:
                        normalise(n + 1)
                    if u in GATED and not last:
                        for part in GATED[u]:
                            gates(n + 1, part)

            dve.memset(partial[:], 0.0)
            dve.memset(eps[:], EPS).then_inc(consts.sem, 1)
            mean_and_variance(dve, STATS, [moments[:, i] for i in range(7)], stats_done)
            dve.wait_ge(sqrt_done.sem, 1)
            dve.reciprocal(rstd[:], std[:]).then_inc(rstd_done.sem, 1)
            dve.wait_ge(rstd_done.sem, 1)
            normalise(0)
            dve.wait_ge(const_in.sem, 48)
            for b in range(2):
                if b == 0:
                    dve.tensor_copy(router[:, 0, :], router32[:]).then_inc(consts.sem, 1)
                else:
                    dve.wait_ge(consts.sem, 2)
                    dve.tensor_tensor(router[:, 1, :], router32[:], router[:, 0, :].bitcast(F32), ALU.subtract).then_inc(consts.sem, 1)
            for i in range(3):
                weight_low(i)
            unscaled_low(0)
            for part in range(4):
                gates(0, part)
            tile(0, True, False)
            with dve.Fori(1, N - 1) as n:
                tile(n, False, False)
            tile(N - 1, False, True)
            h_low(N - 1, U - 1)
            residual(N - 1)


def attention_phase(nc, io, X, STATS, tables):
    D = X.shape[2]
    H, HD = io["M"].shape[0], io["M"].shape[1]
    Q = X.shape[1]
    QPB = 4
    S = QPB * P
    B = Q // QPB
    COLS = P * H
    OCT = P // H
    NO = P // OCT
    JB = 4
    IB = P // JB
    RS, RT = 4, 2
    LAG = 2
    PARTS_OF = ((0,), (1, 2))
    HALF = S // 2
    VW = H * (HD + 1) + 32 - (HD + 1) + 1
    R2 = 2
    HA = 512 // (P // 2)
    UNROLL = 8

    with ExitStack() as ctx:
        def sb(name, shape, dt=F32):
            return ctx.enter_context(nc.sbuf_tensor(f"at_{name}", shape, dt))

        def ps(name, shape, dt=F32):
            return ctx.enter_context(nc.psum_tensor(f"at_{name}", shape, dt))

        def ring(name, per):
            return Ring(ctx.enter_context(nc.semaphore(f"at_{name}")), per)

        ident, wq, wk, wv, wo, bq, bk, bk_far, bv, bo, head_of, pick, window, mz, gate = (
            tables.ident, tables.wq, tables.wk, tables.wv, tables.wo, tables.bq, tables.bk, tables.bk_far, tables.bv,
            tables.bo, tables.head_of, tables.pick, tables.window, tables.mz, tables.gate)
        gate1 = sb("gate1", [P, 1])
        eps, warm = sb("eps", [P, 1]), sb("warm", [P, 1])
        moments = sb("moments", [P, 7, Q, 1])
        mean, var = moments[:, 2], moments[:, 6]
        std, rstd = sb("std", [P, Q, 1]), sb("rstd", [P, Q, 1])
        xn = sb("xn", [P, QPB, D])
        xT = sb("xT", [P, S])
        q32 = sb("q32", [P, S])
        rest = sb("rest", [P, S])
        q_hi, q_lo = sb("q_hi", [P, R2, S], F32R), sb("q_lo", [P, R2, S], F32R)
        q_part = sb("q_part", [P, R2, 3, S], BF16)
        k_hi, k_lo = sb("k_hi", [P, R2, S], F32R), sb("k_lo", [P, R2, S], F32R)
        far_hi, far_lo = sb("far_hi", [P, R2, S], F32R), sb("far_lo", [P, R2, S], F32R)
        v = sb("v", [P, R2, QPB, VW])
        neg = sb("neg", [P, S])
        eneg = rest
        sigma = sb("sigma", [P, R2, S])
        qd_hi = sb("qd_hi", [P, P, H], F32R)
        qd_lo = sb("qd_lo", [P, P, H], F32R)
        qr = sb("qr", [P, R2, COLS], BF16)
        nm = sb("nm", [P, NO])
        expo = sb("expo", [P, RS, S])
        probs = sb("probs", [P, R2, QPB, H, P])
        oc = sb("oc", [P, 512])
        rden = sb("rden", [P, H, 1])
        rdeng = sb("rdeng", [P, H, 1])
        gden = sb("gden", [P, H, 1])
        grden = sb("grden", [P, H, 1])
        grdeng = sb("grdeng", [P, H, 1])
        local, glob, mixed, mixedT = (sb(x, [P, D]) for x in ("local", "glob", "mixed", "mixedT"))
        attended, y = sb("attended", [P, D]), sb("y", [P, D])

        ps_s = ps("ps_s", [P, RS, S])
        ps_t = ps("ps_t", [P, RT, QPB * P])
        ps_v = ps("ps_v", [P, 512])
        misc = ps("misc", [P, 512])

        gate_step, step, stats_done, eps_set = (ring(x, 0) for x in ("gate_step", "step", "stats_done", "eps_set"))
        with nc.Block() as block:
            @block.scalar
            def _(act):
                act.wait_ge(eps_set.sem, 1)
                act.activation(warm[:], eps[:], ACT.Sqrt)
                act.wait_ge(stats_done.sem, 7)
                act.activation(std[:], var, ACT.Sqrt, bias=eps[:, 0:1]).then_inc(step.sem, 1)

            @block.gpsimd
            def _(pool):
                pool.memset(qr[:].rearrange("p r c -> p (r c)").bitcast(U32), 0)
                pool.memset(v[:], 1.0)

            @block.vector
            def _(dve):
                dve.memset(eps[:], EPS).then_inc(eps_set.sem, 1)
                dve.tensor_scalar(gate1[:], gate[:, 1:2], 1.0, None, ALU.add).then_inc(gate_step.sem, 1)
                dve.wait_ge(gate_step.sem, 1)
                dve.reciprocal(gate[:, 2:3], gate1[:]).then_inc(gate_step.sem, 1)
                dve.wait_ge(gate_step.sem, 2)
                dve.tensor_scalar(gate[:, 3:4], gate[:, 2:3], -1.0, 1.0, ALU.mult, ALU.add)
                mean_and_variance(dve, STATS, [moments[:, i] for i in range(7)], stats_done)
                dve.wait_ge(step.sem, 1)
                dve.reciprocal(rstd[:], std[:])

        xn_done = ring("xn_done", 1)
        xT_turned = ring("xT_turned", 1)
        xT_done = ring("xT_done", 1)
        q_proj, k_proj, v_proj = (ring(x, 1) for x in ("q_proj", "k_proj", "v_proj"))
        qhi_done = ring("qhi_done", 1)
        q32_done = ring("q32_done", 1)
        qlo_done = ring("qlo_done", 1)
        split = ring("split", 6)
        neg_exp = ring("neg_exp", 1)
        khi_done, klo_done = ring("khi_done", 1), ring("klo_done", 1)
        v_done = ring("v_done", 1)
        rows_done = ring("rows_done", H // HA)
        even_done = ring("even_done", H // HA)
        odd_done = ring("odd_done", H // HA)
        qdhi_done = ring("qdhi_done", JB)
        qdlo_done = ring("qdlo_done", JB)
        s_done = ring("s_done", NO)
        max_done = ring("max_done", NO)
        exp_done = ring("exp_done", NO)
        t_done = ring("t_done", NO)
        tact_done = ring("tact_done", NO // 2)
        tdve_done = ring("tdve_done", NO // 2)
        pv_done = ring("pv_done", 1)
        oc_done = ring("oc_done", 1)
        o_turned = ring("o_turned", 1)
        o_step = ring("o_step", 3)
        g_prod = ring("g_prod", 1)
        g_step = ring("g_step", 5)
        mixed_turned = ring("mixed_turned", 1)
        mixedT_done = ring("mixedT_done", 1)
        y_prod = ring("y_prod", 1)
        y_done = ring("y_done", 2)

        block = ctx.enter_context(nc.Block())

        def all_steps(eng, step_of):
            first, loops = UNROLL - 3, (Q - UNROLL) // UNROLL
            for c in range(-3, first):
                step_of(0, c)
            with eng.Fori(0, loops) as it:
                for c in range(first, first + UNROLL):
                    step_of(it, c)
            for c in range(first + loops * UNROLL, Q + 2):
                step_of(0, c)

        def at(it, c):
            if isinstance(it, int):
                return c if 0 <= c < Q else None
            return it * UNROLL + c

        def seq(it, c):
            return c // QPB if isinstance(it, int) else it * (UNROLL // QPB) + c // QPB

        def projected(it, c):
            if c % QPB != 1 or at(it, c + 3) is None:
                return None
            return seq(it, c + 3)

        USES = [("A", 0, 0), ("E", 0, 2), ("P", 0, 3), ("E", 1, 5), ("P", 1, 7), ("A", 1, 9), ("P", 2, 10),
                ("E", 2, 12), ("P", 3, 13), ("E", 3, 15)]
        VALUES = (4, 8, 11, 14)

        def present(it, c, kind):
            return {"A": at(it, c + 1), "P": projected(it, c), "E": at(it, c - 2)}[kind] is not None

        def uses(it, c, o):
            return [use for use in USES if use[2] == o and present(it, c, use[0])]

        def turned_at(c, o):
            return (c, o - LAG) if o >= LAG else (c - 1, o - LAG + NO)

        def misc_free(pe, it, c, use):
            i = USES.index(use)
            while True:
                i -= 1
                if i < 0:
                    i, c = len(USES) - 1, c - 1
                    if c < -3:
                        return
                kind, k = USES[i][:2]
                if present(it, c, kind):
                    break
            if kind == "A":
                pe.wait_ge(even_done.sem, even_done.at(at(it, c + 1), k + 1))
                pe.wait_ge(odd_done.sem, odd_done.at(at(it, c + 1), k + 1))
            elif kind == "E":
                q = at(it, c - 2)
                if k == 0:
                    pe.wait_ge(o_step.sem, o_step.at(q, 3))
                elif k == 1:
                    pe.wait_ge(g_step.sem, g_step.at(q, 4))
                elif k == 2:
                    pe.wait_ge(mixedT_done.sem, mixedT_done.at(q, 1))
                else:
                    pe.wait_ge(y_done.sem, y_done.at(q, 1))
            else:
                b = projected(it, c)
                if k == 0:
                    pe.wait_ge(xT_done.sem, xT_done.at(b, 1))
                elif k == 1:
                    pe.wait_ge(qhi_done.sem, qhi_done.at(b, 1))
                    pe.wait_ge(q32_done.sem, q32_done.at(b, 1))
                elif k == 2:
                    pe.wait_ge(klo_done.sem, klo_done.at(b, 1))
                else:
                    pe.wait_ge(v_done.sem, v_done.at(b, 1))

        @block.tensor
        def _(pe):
            def use_a(it, c, k):
                q, b, r = at(it, c), seq(it, c), c // QPB % R2
                pe.wait_ge(split.sem, split.at(b, 6))
                i0 = c % QPB * P
                for g in range(HA):
                    for turn_of in range(2):
                        for band in range(4):
                            parity, parts_of = band // 2, PARTS_OF[band % 2]
                            if turn_of >= len(parts_of):
                                continue
                            part = parts_of[turn_of]
                            rows = slice(32 * band, 32 * band + 32)
                            src = q_part[:, r, part, i0:i0 + P].rearrange("p (i two) -> p i two", two=2)[:, :, parity]
                            ins = pe.matmul(misc[rows, g * (P // 2):(g + 1) * (P // 2)], pick[:, HA * k + g, part, rows], src,
                                            start=(turn_of == 0), stop=(turn_of == len(parts_of) - 1), skip_group_check=True)
                ins.then_inc(rows_done.sem, 1)

            def use_p(it, c, b, k):
                if k == 0:
                    pe.wait_ge(xn_done.sem, xn_done.at(b, 1))
                    for t in range(QPB):
                        ins = pe.transpose(misc[:, t * P:(t + 1) * P], xn[:, t, :], ident[:])
                    ins.then_inc(xT_turned.sem, 1)
                elif k < 3:
                    pe.wait_ge(xT_done.sem, xT_done.at(b, 1))
                    pe.matmul(misc[:], (wq, wk)[k - 1][:], xT[:], start=True, stop=True).then_inc(
                        (q_proj, k_proj)[k - 1].sem, 1)
                else:
                    for t in range(QPB):
                        ins = pe.matmul(misc[:, t * P:(t + 1) * P], xT[:, t * P:(t + 1) * P], wv[:], start=True, stop=True)
                    ins.then_inc(v_proj.sem, 1)

            def use_e(it, c, k):
                q, b, r = at(it, c), seq(it, c), c // QPB % R2
                i0 = c % QPB * P
                if k == 0:
                    pe.wait_ge(oc_done.sem, oc_done.at(q, 1))
                    for s in range(4):
                        ins = pe.transpose(misc[:, s * P:(s + 1) * P], oc[:, s * P:(s + 1) * P], ident[:])
                    ins.then_inc(o_turned.sem, 1)
                elif k == 1:
                    pe.matmul(misc[:, 0:D + H], sigma[:, r, i0:i0 + P], mz[:], start=True, stop=True).then_inc(g_prod.sem, 1)
                elif k == 2:
                    pe.wait_ge(g_step.sem, g_step.at(q, 5))
                    pe.transpose(misc[:, 0:D], mixed[:], ident[:]).then_inc(mixed_turned.sem, 1)
                else:
                    pe.wait_ge(mixedT_done.sem, mixedT_done.at(q, 1))
                    pe.matmul(misc[:, 0:D], mixedT[:], wo[:], start=True, stop=True).then_inc(y_prod.sem, 1)

            def scores(it, c, o):
                q, b, r = at(it, c), seq(it, c), c // QPB % R2
                pe.wait_ge(qdhi_done.sem, qdhi_done.at(q, o * OCT // IB + 1))
                pe.wait_ge(qdlo_done.sem, qdlo_done.at(q, o * OCT // IB + 1))
                if o == 0:
                    pe.wait_ge(klo_done.sem, klo_done.at(b, 1))
                    pe.wait_ge(even_done.sem, even_done.at(q, H // HA))
                    pe.wait_ge(odd_done.sem, odd_done.at(q, H // HA))
                exp_done.wait(pe, q, o + 1 - RS)
                dst = ps_s[:, o % RS, :]
                hi, lo = (x[:, o * OCT:(o + 1) * OCT, :].rearrange("p i h -> p (i h)") for x in (qd_hi, qd_lo))
                place = c % QPB
                runs = {0: ((HALF, S, False), (0, HALF, True)), QPB - 1: ((0, HALF, False), (HALF, S, True))}.get(
                    place, ((0, S, True),))
                for lo_key, hi_key, near in runs:
                    k_h, k_l = ((x[:, r, lo_key:hi_key] for x in ((k_hi, k_lo) if near else (far_hi, far_lo))))
                    out = dst[:, lo_key:hi_key]
                    pe.matmul(out, hi, k_h, start=True, stop=False, skip_group_check=True)
                    pe.matmul(out, hi, k_l, start=False, stop=False, skip_group_check=True)
                    pe.matmul(out, lo, k_h, start=False, stop=not near, skip_group_check=True)
                near_lo, near_hi = [run[:2] for run in runs if run[2]][0]
                for pair in range(4):
                    i = o * OCT + 2 * pair
                    y = S - (place * P + i)
                    ins = pe.matmul(dst[32 * pair:32 * pair + 32, near_lo:near_hi], qr[:, c % R2, i * H:(i + 2) * H],
                                    window[:, y + near_lo:y + near_hi], start=False, stop=(pair == 3), skip_group_check=True)
                ins.then_inc(s_done.sem, 1)

            def turn(it, c, o):
                q = at(it, c)
                pe.wait_ge(exp_done.sem, exp_done.at(q, o + 1))
                if o % 2 == 0:
                    tact_done.wait(pe, q, o // 2)
                else:
                    tdve_done.wait(pe, q, o // 2)
                for kb in range(QPB):
                    ins = pe.transpose(ps_t[:, o % RT, kb * P:(kb + 1) * P], expo[:, o % RS, kb * P:(kb + 1) * P], ident[:])
                ins.then_inc(t_done.sem, 1)

            def values(it, c, j):
                q, b, r = at(it, c), seq(it, c), c // QPB % R2
                if j == 0:
                    pe.wait_ge(tact_done.sem, tact_done.at(q, NO // 2))
                    pe.wait_ge(tdve_done.sem, tdve_done.at(q, NO // 2))
                    pe.wait_ge(v_done.sem, v_done.at(b, 1))
                    oc_done.wait(pe, q, 0)
                for kb in range(QPB):
                    for g in range(4):
                        h = 4 * j + g
                        ins = pe.matmul(ps_v[32 * g:32 * g + 32, j * P:(j + 1) * P],
                                        v[:, r, kb, h * (HD + 1):h * (HD + 1) + 32], probs[:, c % R2, kb, h, :],
                                        start=(kb == 0), stop=(kb == QPB - 1), skip_group_check=True)
                if j == len(VALUES) - 1:
                    ins.then_inc(pv_done.sem, 1)

            def one(it, c):
                for o in range(NO):
                    for use in uses(it, c, o):
                        misc_free(pe, it, c, use)
                        kind, k = use[:2]
                        if kind == "A":
                            use_a(it, c + 1, k)
                        elif kind == "P":
                            use_p(it, c, projected(it, c), k)
                        else:
                            use_e(it, c - 2, k)
                    if at(it, c) is not None:
                        scores(it, c, o)
                    ct, ot = turned_at(c, o)
                    if at(it, ct) is not None:
                        turn(it, ct, ot)
                    if o in VALUES and at(it, c - 1) is not None:
                        values(it, c - 1, VALUES.index(o))
            all_steps(pe, one)

        def turned_to_probs(eng, copy, it, c, o, done):
            q = at(it, c)
            eng.wait_ge(t_done.sem, t_done.at(q, o + 1))
            if o < 2:
                pv_done.wait(eng, q, -1)
            dst = probs[:, c % R2, :, :, o * OCT:(o + 1) * OCT]
            copy(dst, ps_t[:, o % RT, :].rearrange("p (k i h) -> p k h i", k=QPB, h=H)).then_inc(done.sem, 1)

        @block.scalar
        def _(act):
            def use_a(it, c, k):
                q = at(it, c)
                act.wait_ge(rows_done.sem, rows_done.at(q, k + 1))
                if k == 0:
                    s_done.wait(act, q, -NO)
                src = misc[0:ODD, :].rearrange("p (g i) -> p g i", g=HA)
                dst = qr[0:ODD, c % R2, :].rearrange("p (i two h) -> p h i two", two=2, h=H)
                act.copy(dst[:, HA * k:HA * (k + 1), :, 0], src).then_inc(even_done.sem, 1)

            def use_p(it, c, b, k):
                r = (c + 3) // QPB % R2
                if k == 0:
                    act.wait_ge(xT_turned.sem, xT_turned.at(b, 1))
                    v_proj.wait(act, b, 0)
                    act.copy(xT[:], misc[:]).then_inc(xT_done.sem, 1)
                elif k == 1:
                    act.wait_ge(q_proj.sem, q_proj.at(b, 1))
                    qdhi_done.wait(act, at(it, c + 3), -JB * QPB)
                    act.activation(q_hi[:, r, :], misc[:], ACT.Identity, bias=bq[:, 0:1]).then_inc(qhi_done.sem, 1)
                elif k == 2:
                    act.wait_ge(k_proj.sem, k_proj.at(b, 1))
                    s_done.wait(act, at(it, c + 3), -NO * QPB)
                    act.activation(k_hi[:, r, :], misc[:], ACT.Identity, bias=bk[:, 0:1])
                    for end, keys in enumerate((slice(0, HALF), slice(HALF, S))):
                        ins = act.activation(far_hi[:, r, keys], misc[:, keys], ACT.Identity, bias=bk_far[:, end:end + 1])
                    ins.then_inc(khi_done.sem, 1)

            def one(it, c):
                for o in range(NO):
                    for kind, k, _ in uses(it, c, o):
                        if kind == "A":
                            use_a(it, c + 1, k)
                        elif kind == "P":
                            use_p(it, c, projected(it, c), k)
                        elif kind == "E" and k == 2:
                            q = at(it, c - 2)
                            act.wait_ge(mixed_turned.sem, mixed_turned.at(q, 1))
                            y_prod.wait(act, q, 0)
                            act.copy(mixedT[:], misc[:, 0:D]).then_inc(mixedT_done.sem, 1)
                    q = at(it, c)
                    if q is not None:
                        act.wait_ge(max_done.sem, max_done.at(q, o + 1))
                        t_done.wait(act, q, o + 1 - RS)
                        act.activation(expo[:, o % RS, :], ps_s[:, o % RS, :], ACT.Exp,
                                       bias=nm[:, o:o + 1]).then_inc(exp_done.sem, 1)
                    ct, ot = turned_at(c, o)
                    if ot % 2 == 0 and at(it, ct) is not None:
                        turned_to_probs(act, act.copy, it, ct, ot, tact_done)
                    if o == 13 and projected(it, c) is not None:
                        b = projected(it, c)
                        act.wait_ge(split.sem, split.at(b, 5))
                        act.activation(eneg[:], neg[:], ACT.Exp).then_inc(neg_exp.sem, 1)
            all_steps(act, one)

        @block.gpsimd
        def _(pool):
            heads = head_of[:].rearrange("p (a h) -> p a h", a=1).broadcast_to([P, IB, H])

            def expand(it, c, jb, src, dst, done):
                i0 = c % QPB * P + jb * IB
                x = src[:, c // QPB % R2, i0:i0 + IB].bitcast(F32).rearrange("p (i a) -> p i a", a=1).broadcast_to([P, IB, H])
                pool.tensor_tensor(dst[:, jb * IB:(jb + 1) * IB, :], x, heads, ALU.mult).then_inc(done.sem, 1)

            def one(it, c):
                b = projected(it, c)
                q = at(it, c + 1)
                for jb in range(JB):
                    if q is not None:
                        pool.wait_ge(qlo_done.sem, qlo_done.at(seq(it, c + 1), 1))
                        s_done.wait(pool, q, -NO + (jb + 1) * NO // JB)
                        expand(it, c + 1, jb, q_hi, qd_hi, qdhi_done)
                        expand(it, c + 1, jb, q_lo, qd_lo, qdlo_done)
                if b is not None:
                    r = (c + 3) // QPB % R2
                    pool.wait_ge(q32_done.sem, q32_done.at(b, 1))
                    pool.wait_ge(qhi_done.sem, qhi_done.at(b, 1))
                    pool.tensor_tensor(q_lo[:, r, :], q32[:], q_hi[:, r, :].bitcast(F32), ALU.subtract).then_inc(qlo_done.sem, 1)
            all_steps(pool, one)

        @block.vector
        def _(dve):
            def use_a(it, c, k):
                q = at(it, c)
                dve.wait_ge(rows_done.sem, rows_done.at(q, k + 1))
                if k == 0:
                    s_done.wait(dve, q, -NO)
                src = misc[ODD:P, :].rearrange("p (g i) -> p g i", g=HA)
                dst = qr[ODD:P, c % R2, :].rearrange("p (i two h) -> p h i two", two=2, h=H)
                dve.tensor_copy(dst[:, HA * k:HA * (k + 1), :, 1], src).then_inc(odd_done.sem, 1)

            def use_p(it, c, b, k):
                r = (c + 3) // QPB % R2
                if k == 1:
                    dve.wait_ge(q_proj.sem, q_proj.at(b, 1))
                    qlo_done.wait(dve, b, 0)
                    dve.wait_ge(qhi_done.sem, qhi_done.at(b, 1))
                    dve.tensor_scalar(q32[:], misc[:], bq[:, 0:1], None, ALU.add).then_inc(q32_done.sem, 1)
                elif k == 2:
                    dve.wait_ge(khi_done.sem, khi_done.at(b, 1))
                    dve.scalar_tensor_tensor(out=k_lo[:, r, :], in0=misc[:], scalar=bk[:, 0:1],
                                             in1=k_hi[:, r, :].bitcast(F32), op0=ALU.add, op1=ALU.subtract)
                    for end, keys in enumerate((slice(0, HALF), slice(HALF, S))):
                        ins = dve.scalar_tensor_tensor(out=far_lo[:, r, keys], in0=misc[:, keys], scalar=bk_far[:, end:end + 1],
                                                       in1=far_hi[:, r, keys].bitcast(F32), op0=ALU.add, op1=ALU.subtract)
                    ins.then_inc(klo_done.sem, 1)
                elif k == 3:
                    dve.wait_ge(v_proj.sem, v_proj.at(b, 1))
                    pv_done.wait(dve, at(it, c + 3), -QPB)
                    dst = v[:, r, :, 0:H * (HD + 1)].rearrange("p t (h e) -> p t h e", h=H)[:, :, :, 0:HD]
                    bias = bv[:].rearrange("p (t h e) -> p t h e", t=1, h=H).broadcast_to([P, QPB, H, HD])
                    dve.tensor_tensor(dst, misc[:].rearrange("p (t h e) -> p t h e", t=QPB, h=H), bias,
                                      ALU.add).then_inc(v_done.sem, 1)

            def query_parts(it, c, b):
                r = (c + 3) // QPB % R2
                dve.wait_ge(q32_done.sem, q32_done.at(b, 1))
                rows_done.wait(dve, at(it, c + 3), -(H // HA) * QPB)
                dve.tensor_copy(q_part[:, r, 0, :], q32[:]).then_inc(split.sem, 1)
                dve.wait_ge(split.sem, split.at(b, 1))
                dve.tensor_tensor(rest[:], q32[:], q_part[:, r, 0, :], ALU.subtract).then_inc(split.sem, 1)
                dve.wait_ge(split.sem, split.at(b, 2))
                dve.tensor_copy(q_part[:, r, 1, :], rest[:]).then_inc(split.sem, 1)
                dve.wait_ge(split.sem, split.at(b, 3))
                dve.tensor_tensor(q_part[:, r, 2, :], rest[:], q_part[:, r, 1, :], ALU.subtract).then_inc(split.sem, 1)
                dve.tensor_scalar(neg[:], q32[:], 0.0, None, ALU.min).then_inc(split.sem, 1)

            def finish_sigma(it, c, b):
                r = (c + 3) // QPB % R2
                dve.wait_ge(neg_exp.sem, neg_exp.at(b, 1))
                g_prod.wait(dve, at(it, c + 3), -QPB)
                dve.scalar_tensor_tensor(out=sigma[:, r, :], in0=q32[:], scalar=0.0, in1=eneg[:], op0=ALU.max,
                                         op1=ALU.add).then_inc(split.sem, 1)

            def use_e(it, c, k):
                q = at(it, c)
                turned = misc[:].rearrange("p (h e) -> p h e", e=32)
                by_head = lambda x: x[:].rearrange("p (h e) -> p h e", h=H)
                spreadh = lambda x: x[:].broadcast_to([P, H, HD])
                if k == 0:
                    dve.wait_ge(o_turned.sem, o_turned.at(q, 1))
                    g_step.wait(dve, q, 0)
                    dve.reciprocal(rden[:], turned[:, :, HD:HD + 1]).then_inc(o_step.sem, 1)
                    dve.wait_ge(o_step.sem, o_step.at(q, 1))
                    dve.tensor_scalar(rdeng[:], rden[:], gate[:, 2:3], None, ALU.mult).then_inc(o_step.sem, 1)
                    dve.wait_ge(o_step.sem, o_step.at(q, 2))
                    dve.tensor_tensor(by_head(local), turned[:, :, 0:HD], spreadh(rdeng), ALU.mult).then_inc(o_step.sem, 1)
                elif k == 1:
                    dve.wait_ge(g_prod.sem, g_prod.at(q, 1))
                    dve.tensor_scalar(gden[:], misc[:, D:D + H], 1e-6, None, ALU.add).then_inc(g_step.sem, 1)
                    dve.wait_ge(g_step.sem, g_step.at(q, 1))
                    dve.reciprocal(grden[:], gden[:]).then_inc(g_step.sem, 1)
                    dve.wait_ge(g_step.sem, g_step.at(q, 2))
                    dve.tensor_scalar(grdeng[:], grden[:], gate[:, 3:4], None, ALU.mult).then_inc(g_step.sem, 1)
                    dve.wait_ge(g_step.sem, g_step.at(q, 3))
                    dve.tensor_tensor(by_head(glob), misc[:, 0:D].rearrange("p (h e) -> p h e", h=H), spreadh(grdeng),
                                      ALU.mult).then_inc(g_step.sem, 1)
                    g_step.wait(dve, q, 4)
                    mixed_turned.wait(dve, q, 0)
                    dve.tensor_tensor(mixed[:], local[:], glob[:], ALU.add).then_inc(g_step.sem, 1)
                elif k == 3:
                    row = X[:, bass.ds(q, 1), :].rearrange("p a d -> p (a d)")
                    dve.wait_ge(y_prod.sem, y_prod.at(q, 1))
                    dve.tensor_tensor(attended[:], misc[:, 0:D], bo[:], ALU.add).then_inc(y_done.sem, 1)
                    dve.wait_ge(y_done.sem, y_done.at(q, 1))
                    dve.tensor_tensor(y[:], attended[:], row, ALU.add).then_inc(y_done.sem, 1)
                    dve.wait_ge(y_done.sem, y_done.at(q, 2))
                    dve.tensor_scalar(row, y[:], 0.0, None, ALU.add)
                    dve.bn_stats(STATS[:, bass.ds(q, 1), :].rearrange("p a d -> p (a d)"), y[:])

            def maximum(it, c, o):
                q = at(it, c)
                dve.wait_ge(s_done.sem, s_done.at(q, o + 1))
                dve.tensor_reduce(nm[:, o:o + 1], ps_s[:, o % RS, :], AX.X, ALU.max, negate=True).then_inc(max_done.sem, 1)

            def one(it, c):
                b = projected(it, c)
                if b is not None:
                    xT_turned.wait(dve, b, 0)
                    for t in range(QPB):
                        row = at(it, c + 3 + t)
                        ins = dve.tensor_scalar(xn[:, t, :], X[:, bass.ds(row, 1), :].rearrange("p a d -> p (a d)"),
                                                mean[:, bass.ds(row, 1), :].rearrange("p a d -> p (a d)"),
                                                rstd[:, bass.ds(row, 1), :].rearrange("p a d -> p (a d)"),
                                                ALU.subtract, ALU.mult)
                    ins.then_inc(xn_done.sem, 1)
                q = at(it, c - 2)
                if q is not None:
                    dve.wait_ge(pv_done.sem, pv_done.at(q, 1))
                    o_turned.wait(dve, q, 0)
                    dve.tensor_copy(oc[:], ps_v[:]).then_inc(oc_done.sem, 1)
                for o in range(NO):
                    for kind, k, _ in uses(it, c, o):
                        if kind == "A":
                            use_a(it, c + 1, k)
                        elif kind == "P":
                            use_p(it, c, b, k)
                        else:
                            use_e(it, c - 2, k)
                    if at(it, c) is not None:
                        maximum(it, c, o)
                    ct, ot = turned_at(c, o)
                    if ot % 2 == 1 and at(it, ct) is not None:
                        turned_to_probs(dve, dve.tensor_copy, it, ct, ot, tdve_done)
                    if b is not None and o == 11:
                        query_parts(it, c, b)
                    if b is not None and o == 15:
                        finish_sigma(it, c, b)
            all_steps(dve, one)


ROWS = (((1, 1), (1, 2), (1, 3)), ((2, 1), (2, 2), (3, 1)))
ODD = 64


class Buffers:
    pass


def attention_tables(nc, ctx, io):
    D, H, S = io["x"].shape[2], io["M"].shape[0], 4 * P

    def sb(name, shape, dt=F32):
        return ctx.enter_context(nc.sbuf_tensor(f"tab_{name}", shape, dt))

    tables = Buffers()
    tables.ident = sb("ident", [P, P])
    tables.wq, tables.wk, tables.wv, tables.wo = (sb(w, [P, D]) for w in ("wq", "wk", "wv", "wo"))
    tables.bq, tables.bk = sb("bq", [P, 1]), sb("bk", [P, 1])
    tables.bk_far = sb("bk_far", [P, 2])
    tables.bv, tables.bo = sb("bv", [P, D]), sb("bo", [P, D])
    tables.head_of = sb("head_of", [P, H])
    tables.pick = sb("pick", [P, H, 3, P], BF16)
    tables.window = sb("window", [P, 2 * S], BF16)
    tables.mz = sb("mz", [P, D + H])
    tables.gate = sb("gate", [P, 4])
    return tables


def table_scratch(nc, ctx, io):
    NREL = io["rel"].shape[1]

    def sb(name, shape, dt=F32):
        return ctx.enter_context(nc.sbuf_tensor(f"scr_{name}", shape, dt))

    def signal(name):
        return ctx.enter_context(nc.semaphore(f"scr_{name}"))

    scratch = Buffers()
    scratch.rel = sb("rel", [P, NREL])
    scratch.rel_rest = sb("rel_rest", [P, NREL])
    scratch.rel_part = sb("rel_part", [P, 3, NREL], BF16)
    scratch.rel_row = sb("rel_row", [P, NREL])
    scratch.emb_part = sb("emb_part", [P, 3])
    scratch.spread32, scratch.spread = sb("spread32", [P, 3, P]), sb("spread", [P, 3, P], BF16)
    scratch.m_sb, scratch.z_sb = sb("m_sb", [P, io["M"].shape[1]]), sb("z_sb", [P, 1])
    scratch.scaled, scratch.split_rel, scratch.chosen, scratch.spread_done = (
        signal(x) for x in ("scaled", "split_rel", "chosen", "spread_done"))
    return scratch


def table_steps(dve, io, tables, scratch, u):
    window, mz, head_of, bk, wk = tables.window, tables.mz, tables.head_of, tables.bk, tables.wk
    rel_rest, rel_part, rel_row, emb_part = scratch.rel_rest, scratch.rel_part, scratch.rel_row, scratch.emb_part
    H, HD = io["M"].shape[0], io["M"].shape[1]
    D, S, SCALE = io["x"].shape[2], 4 * P, float(HD) ** -0.5
    NREL = io["rel"].shape[1]
    REL = NREL // 2
    if u == 0:
        dve.memset(window[:].bitcast(U32), 0)
        dve.tensor_scalar(bk[:], bk[:], SCALE, None, ALU.mult)
        dve.tensor_scalar(rel_rest[:], scratch.rel[:], SCALE, None, ALU.mult).then_inc(scratch.scaled, 1)
        dve.tensor_copy(scratch.spread[:], scratch.spread32[:]).then_inc(scratch.spread_done, 1)
    elif u == 1:
        dve.tensor_scalar(wk[:], wk[:], SCALE, None, ALU.mult)
        dve.wait_ge(scratch.scaled, 1)
        for end in range(2):
            dve.tensor_tensor(tables.bk_far[:, end:end + 1], bk[:], rel_rest[:, 2 * REL * end:2 * REL * end + 1], ALU.add)
    elif u < 5:
        i = u - 2
        if i > 0:
            dve.wait_ge(scratch.split_rel, 2 * i)
        dve.tensor_copy(rel_part[:, i], rel_rest[:]).then_inc(scratch.split_rel, 1)
        dve.wait_ge(scratch.split_rel, 2 * i + 1)
        dve.tensor_tensor(rel_rest[:], rel_rest[:], rel_part[:, i], ALU.subtract).then_inc(scratch.split_rel, 1)
    elif u == 5:
        dve.tensor_scalar(rel_row[:], rel_part[:, 0], emb_part[:, 0:1], None, ALU.mult).then_inc(scratch.chosen, 1)
        for i in (1, 2):
            dve.wait_ge(scratch.chosen, i)
            dve.scalar_tensor_tensor(out=rel_row[:], in0=rel_part[:, i], scalar=emb_part[:, i:i + 1], in1=rel_row[:],
                                     op0=ALU.mult, op1=ALU.add).then_inc(scratch.chosen, 1)
    elif u < 8:
        dve.wait_ge(scratch.chosen, 3)
        par = u - 6
        rows = slice(ODD * par, ODD * par + ODD)
        at = S - REL + par
        dve.tensor_copy(window[rows, at:at + NREL], rel_row[rows, :])
        dve.tensor_scalar(window[rows, 0:at], window[rows, 0:at], rel_row[rows, 0:1], None, ALU.add)
        dve.tensor_scalar(window[rows, at + NREL:2 * S], window[rows, at + NREL:2 * S],
                          rel_row[rows, NREL - 1:NREL], None, ALU.add)
    elif u < 16:
        dve.wait_ge(scratch.spread_done, 1)
        for h in range((u - 8) * H // 8, (u - 7) * H // 8):
            dve.tensor_scalar(tables.pick[:, h], scratch.spread[:], head_of[:, h:h + 1], None, ALU.mult)
    elif u == 16:
        dve.tensor_tensor(mz[:, 0:D].rearrange("p (h v) -> p h v", h=H),
                          head_of[:].rearrange("p (h a) -> p h a", a=1).broadcast_to([P, H, HD]),
                          scratch.m_sb[:].rearrange("p (a v) -> p a v", a=1).broadcast_to([P, H, HD]), ALU.mult)
        dve.tensor_scalar(mz[:, D:D + H], head_of[:], scratch.z_sb[:, 0:1], None, ALU.mult)


def load_phase(nc, io, X, STATS, tables, scratch):
    ROWS_OF_X = X.shape[1]
    PIECE = 4
    PIECES = ROWS_OF_X // PIECE
    with ExitStack() as ctx:
        def signal(name):
            return ctx.enter_context(nc.semaphore(f"load_{name}"))

        x_in = [signal(f"x_in{k}") for k in range(PIECES)]
        const_in = signal("const_in")
        loads = [(tables.gate[:, 0:1], io["alpha"]), (scratch.m_sb[:], io["M"].rearrange("h d v -> (h d) v"))] + [
            (to[:], io[name]) for to, name in (
                (scratch.rel, "rel"), (scratch.emb_part, "emb_part"), (scratch.spread32, "spread"), (scratch.z_sb, "z"),
                (tables.head_of, "head_of"), (tables.ident, "ident"), (tables.wk, "wk"), (tables.bk, "bk"),
                (tables.wq, "wq"), (tables.bq, "bq"), (tables.wv, "wv"), (tables.bv, "bv"), (tables.wo, "wo"),
                (tables.bo, "bo"))]
        block = ctx.enter_context(nc.Block())

        @block.sync
        def _(sp):
            for i in range(PIECES):
                sp.dma_start(X[:, i * PIECE:(i + 1) * PIECE, :], io["x"][:, i * PIECE:(i + 1) * PIECE, :]).then_inc(x_in[i], 16)

        @block.scalar
        def _(act):
            for to, src in loads:
                act.dma_start(to, src).then_inc(const_in, 16)
            act.wait_ge(const_in, 16 * len(loads))
            act.activation(tables.gate[:, 1:2], tables.gate[:, 0:1], ACT.Exp, scale=-1.0)

        @block.vector
        def _(dve):
            for i in range(PIECES):
                dve.wait_ge(x_in[i], 16)
                for t in range(PIECE):
                    dve.bn_stats(STATS[:, i * PIECE + t, :], X[:, i * PIECE + t, :])


def macaron_layer(nc, io, out):
    D = io["x"].shape[2]
    ROWS = io["x"].shape[1]
    with ExitStack() as ctx:
        X = ctx.enter_context(nc.sbuf_tensor("X", [P, ROWS, D], F32))
        STATS = ctx.enter_context(nc.sbuf_tensor("STATS", [P, ROWS, 6], F32))
        tables = attention_tables(nc, ctx, io)
        with ExitStack() as early:
            scratch = table_scratch(nc, early, io)
            load_phase(nc, io, X, STATS, tables, scratch)
            ffn_phase(nc, io, X, STATS, "ffn1", None, lambda dve, u: table_steps(dve, io, tables, scratch, u))
        attention_phase(nc, io, X, STATS, tables)
        ffn_phase(nc, io, X, STATS, "ffn2", out)


def _shape_constants():
    import numpy as _np

    heads, hd = 16, 8
    bands = (((1, 1), (1, 2), (1, 3)), ((2, 1), (2, 2), (3, 1))) * 2
    head_of = _np.kron(_np.eye(heads), _np.ones((hd, 1))).astype(_np.float32)
    spread = _np.zeros((128, 3, 128), _np.float32)
    emb_part = _np.zeros((128, 3), _np.float32)
    for band in range(4):
        for n, (q_part, e_part) in enumerate(bands[band]):
            for d in range(hd):
                row = 32 * band + hd * n + d
                spread[d::hd, q_part - 1, row] = 1.0
                emb_part[row, e_part - 1] = 1.0
    return {"head_of": head_of, "spread": spread, "emb_part": emb_part}


def kernel(**inputs):
    import numpy as _np
    import concourse.bacc as _bacc
    from concourse import mybir as _mybir
    from concourse.bass_utils import run_bass_kernel_spmd as _run

    nc = _bacc.Bacc("TRN2", target_bir_lowering=False, num_devices=1)
    x = _np.asarray(inputs["L0_attn_hidden_states"])
    f, a = "L0_ffn_", "L0_attn_"
    host = {
        "x": x.reshape(-1, 128, x.shape[-1]),
        "router": inputs[f + "router_DE"],
        "w_in": inputs[f + "w_in_eDF"],
        "w_gate": inputs[f + "w_swiglu_eDF"],
        "w_out": inputs[f + "w_out_eFD"],
        "w_in_s": _np.asarray(inputs[f + "w_in_shared_FD"]).T,
        "w_gate_s": _np.asarray(inputs[f + "w_swiglu_FD"]).T,
        "w_out_s": _np.asarray(inputs[f + "w_out_shared_DF"]).T,
        "ident": _np.eye(128, dtype=_np.float32),
        "wq": _np.asarray(inputs[a + "Wq"]).T,
        "wk": _np.asarray(inputs[a + "Wk"]).T,
        "wv": _np.asarray(inputs[a + "Wv"]).T,
        "wo": _np.asarray(inputs[a + "Wo"]).T,
        "bq": _np.asarray(inputs[a + "bq"]).reshape(128, 1),
        "bk": _np.asarray(inputs[a + "bk"]).reshape(128, 1),
        "bv": _np.asarray(inputs[a + "bv"]).reshape(1, 128),
        "bo": _np.asarray(inputs[a + "bo"]).reshape(1, 128),
        "M": inputs[a + "M"],
        "z": _np.asarray(inputs[a + "z"]).reshape(128, 1),
        "alpha": _np.asarray(inputs[a + "gate_alpha"]).reshape(1, 1),
        "rel": _np.tile(_np.asarray(inputs[a + "rel_emb"])[::-1].T, (16, 1)),
        **_shape_constants(),
        "ranks": _np.tile(_np.arange(8, 0, -1, dtype=_np.float32), (128, 4, 1)),
    }
    arrays, io = {}, {}
    for name, a in host.items():
        a = _np.ascontiguousarray(a)
        arrays["in_" + name] = a
        io[name] = nc.dram_tensor("in_" + name, a.shape, _mybir.dt.from_np(a.dtype), kind="ExternalInput").ap()
    io["alpha"] = io["alpha"].broadcast_to([128, 1])
    io["bv"], io["bo"] = (io[bias].broadcast_to([128, 128]) for bias in ("bv", "bo"))
    io["x"] = io["x"].rearrange("r p d -> p r d")
    out = nc.dram_tensor("out_0", x.shape, _mybir.dt.float32, kind="ExternalOutput").ap()
    macaron_layer(nc, io, out.rearrange("b (r p) d -> p (b r) d", p=128))
    r = _run(nc, [arrays], core_ids=[0])
    return r.results[0]["out_0"]
```
